# Optimizing a Trainium2 kernel written in Bass

```python
import numpy as np
import jax
import jax.numpy as jnp

def _softmax(x, axis=-1):
    return jax.nn.softmax(x, axis=axis)

def _gelu(x):
    return jax.nn.gelu(x, approximate=True)

def _silu(x):
    return jax.nn.silu(x)

def _sigmoid(x):
    return jax.nn.sigmoid(x)

def _layernorm(x, axis=-1, eps=1e-05):
    m = jnp.mean(x, axis=axis, keepdims=True)
    v = jnp.var(x, axis=axis, keepdims=True)
    return (x - m) / jnp.sqrt(v + eps)

def _scatter_add(tgt, idx, src, axis=0):
    return tgt.at[idx].add(src)

def _segment_sum(src, seg, n):
    return jax.ops.segment_sum(src, seg, n)
kernel_name = 'mk_conv_seq_d1_conv_nhwc96_r2_b53883'

def setup_inputs(seed: int=0):
    np.random.seed(seed)
    _w = jnp.asarray

    def _rec_inputs():
        import jax
        import jax.numpy as jnp
        _gk = jax.random.key(seed)
        x = -0.0002221 + 1 * jax.random.normal(jax.random.fold_in(_gk, 1), (4, 128, 128, 48), jnp.float32)
        return x
    x = _rec_inputs()

    def _L0_conv_setup():
        import jax, jax.numpy as jnp
        import numpy as np
        B, H, W, C = (4, 128, 128, 48)
        WIN = 8
        HEADS = 3
        HD = C // HEADS
        SCALE = HD ** (-0.5)
        N = WIN * WIN
        HID = 4 * C

        def _rel_pos_index(w):
            coords = np.stack(np.meshgrid(np.arange(w), np.arange(w), indexing='ij')).reshape(2, -1)
            rel = coords[:, :, None] - coords[:, None, :]
            rel = rel.transpose(1, 2, 0).astype(np.int64)
            rel[:, :, 0] += w - 1
            rel[:, :, 1] += w - 1
            rel[:, :, 0] *= 2 * w - 1
            return jnp.asarray(rel.sum(-1))
        REL_IDX = _rel_pos_index(WIN)

        def layernorm(x, g, b, eps=1e-05):
            mu = jnp.mean(x, -1, keepdims=True)
            var = jnp.mean(jnp.square(x - mu), -1, keepdims=True)
            return (x - mu) * jax.lax.rsqrt(var + eps) * g + b
        key = jax.random.key(seed)
        ks = jax.random.split(key, 8)
        s = 0.02
        return {'x': jax.random.normal(ks[0], (B, H, W, C), jnp.float32), 'norm1_g': jnp.ones((C,), jnp.float32), 'norm1_b': jnp.zeros((C,), jnp.float32), 'qkv_w': jax.random.normal(ks[1], (C, 3 * C), jnp.float32) * s, 'qkv_b': jnp.zeros((3 * C,), jnp.float32), 'proj_w': jax.random.normal(ks[2], (C, C), jnp.float32) * s, 'proj_b': jnp.zeros((C,), jnp.float32), 'rel_bias_table': jax.random.normal(ks[3], ((2 * WIN - 1) ** 2, HEADS), jnp.float32) * s, 'norm2_g': jnp.ones((C,), jnp.float32), 'norm2_b': jnp.zeros((C,), jnp.float32), 'fc1_w': jax.random.normal(ks[4], (C, HID), jnp.float32) * s, 'fc1_b': jnp.zeros((HID,), jnp.float32), 'fc2_w': jax.random.normal(ks[5], (HID, C), jnp.float32) * s, 'fc2_b': jnp.zeros((C,), jnp.float32)}
    _L0_conv_all = _L0_conv_setup()
    _L0_conv_in = {k: v for k, v in _L0_conv_all.items() if k in ('norm1_g', 'norm1_b', 'qkv_w', 'qkv_b', 'proj_w', 'proj_b', 'rel_bias_table', 'norm2_g', 'norm2_b', 'fc1_w', 'fc1_b', 'fc2_w', 'fc2_b')}
    del _L0_conv_all
    return {'x': x, 'L0_conv_norm1_g': _L0_conv_in['norm1_g'], 'L0_conv_norm1_b': _L0_conv_in['norm1_b'], 'L0_conv_qkv_w': _L0_conv_in['qkv_w'], 'L0_conv_qkv_b': _L0_conv_in['qkv_b'], 'L0_conv_proj_w': _L0_conv_in['proj_w'], 'L0_conv_proj_b': _L0_conv_in['proj_b'], 'L0_conv_rel_bias_table': _L0_conv_in['rel_bias_table'], 'L0_conv_norm2_g': _L0_conv_in['norm2_g'], 'L0_conv_norm2_b': _L0_conv_in['norm2_b'], 'L0_conv_fc1_w': _L0_conv_in['fc1_w'], 'L0_conv_fc1_b': _L0_conv_in['fc1_b'], 'L0_conv_fc2_w': _L0_conv_in['fc2_w'], 'L0_conv_fc2_b': _L0_conv_in['fc2_b']}

def reference(x, L0_conv_norm1_g, L0_conv_norm1_b, L0_conv_qkv_w, L0_conv_qkv_b, L0_conv_proj_w, L0_conv_proj_b, L0_conv_rel_bias_table, L0_conv_norm2_g, L0_conv_norm2_b, L0_conv_fc1_w, L0_conv_fc1_b, L0_conv_fc2_w, L0_conv_fc2_b):
    import jax
    import jax.numpy as jnp

    def _L0_conv_ref(x, norm1_g, norm1_b, qkv_w, qkv_b, proj_w, proj_b, rel_bias_table, norm2_g, norm2_b, fc1_w, fc1_b, fc2_w, fc2_b):
        import jax, jax.numpy as jnp
        import numpy as np
        B, H, W, C = (4, 128, 128, 48)
        WIN = 8
        HEADS = 3
        HD = C // HEADS
        SCALE = HD ** (-0.5)
        N = WIN * WIN
        HID = 4 * C

        def _rel_pos_index(w):
            coords = np.stack(np.meshgrid(np.arange(w), np.arange(w), indexing='ij')).reshape(2, -1)
            rel = coords[:, :, None] - coords[:, None, :]
            rel = rel.transpose(1, 2, 0).astype(np.int64)
            rel[:, :, 0] += w - 1
            rel[:, :, 1] += w - 1
            rel[:, :, 0] *= 2 * w - 1
            return jnp.asarray(rel.sum(-1))
        REL_IDX = _rel_pos_index(WIN)

        def layernorm(x, g, b, eps=1e-05):
            mu = jnp.mean(x, -1, keepdims=True)
            var = jnp.mean(jnp.square(x - mu), -1, keepdims=True)
            return (x - mu) * jax.lax.rsqrt(var + eps) * g + b
        shortcut = x
        h = layernorm(x, norm1_g, norm1_b)
        hw = h.reshape(B, H // WIN, WIN, W // WIN, WIN, C)
        hw = hw.transpose(0, 1, 3, 2, 4, 5).reshape(-1, N, C)
        Bw = hw.shape[0]
        qkv = hw @ qkv_w + qkv_b
        qkv = qkv.reshape(Bw, N, 3, HEADS, HD)
        q = jnp.transpose(qkv[:, :, 0], (0, 2, 1, 3))
        k = jnp.transpose(qkv[:, :, 1], (0, 2, 1, 3))
        v = jnp.transpose(qkv[:, :, 2], (0, 2, 1, 3))
        attn = jnp.einsum('bhnd,bhmd->bhnm', q * SCALE, k)
        bias = rel_bias_table[REL_IDX].transpose(2, 0, 1)
        attn = jax.nn.softmax(attn + bias[None], axis=-1)
        out = jnp.einsum('bhnm,bhmd->bhnd', attn, v)
        out = out.transpose(0, 2, 1, 3).reshape(Bw, N, C)
        out = out @ proj_w + proj_b
        out = out.reshape(B, H // WIN, W // WIN, WIN, WIN, C)
        out = out.transpose(0, 1, 3, 2, 4, 5).reshape(B, H, W, C)
        x = shortcut + out
        h2 = layernorm(x, norm2_g, norm2_b)
        mlp = jax.nn.gelu(h2 @ fc1_w + fc1_b, approximate=False) @ fc2_w + fc2_b
        return x + mlp

    def _gn(v, G=32, eps=1e-05):
        B_, H_, W_, C_ = v.shape
        g = v.reshape(B_, H_, W_, G, C_ // G)
        m = jnp.mean(g, axis=(1, 2, 4), keepdims=True)
        s = jnp.var(g, axis=(1, 2, 4), keepdims=True)
        return ((g - m) / jnp.sqrt(s + eps)).reshape(v.shape)

    def _ln_c(v, eps=1e-06):
        m = jnp.mean(v, axis=-1, keepdims=True)
        s = jnp.var(v, axis=-1, keepdims=True)
        return (v - m) / jnp.sqrt(s + eps)

    def _ln_t(v, eps=1e-05):
        m = jnp.mean(v, axis=-1, keepdims=True)
        s = jnp.var(v, axis=-1, keepdims=True)
        return (v - m) / jnp.sqrt(s + eps)

    def _to_tokens(v):
        B_, H_, W_, C_ = v.shape
        return v.reshape(B_, H_ * W_, C_)

    def _from_tokens(t, like):
        return t.reshape(like.shape)
    x = _L0_conv_ref(x, L0_conv_norm1_g, L0_conv_norm1_b, L0_conv_qkv_w, L0_conv_qkv_b, L0_conv_proj_w, L0_conv_proj_b, L0_conv_rel_bias_table, L0_conv_norm2_g, L0_conv_norm2_b, L0_conv_fc1_w, L0_conv_fc1_b, L0_conv_fc2_w, L0_conv_fc2_b)
    return x

_drawn_inputs = setup_inputs


def setup_inputs(seed=0):
    import zlib

    import numpy as np

    out = dict(_drawn_inputs(seed))
    spreads = {'L0_conv_norm1_g': (1.0, 0.6),
     'L0_conv_norm1_b': (0.0, 0.8),
     'L0_conv_qkv_b': (0.0, 0.715),
     'L0_conv_proj_b': (0.0, 0.1),
     'L0_conv_norm2_g': (1.0, 0.6),
     'L0_conv_norm2_b': (0.0, 0.8),
     'L0_conv_fc1_b': (0.0, 0.447),
     'L0_conv_fc2_b': (0.0, 0.1)}
    factors = {'L0_conv_qkv_w': 8.0,
     'L0_conv_proj_w': 5.56,
     'L0_conv_rel_bias_table': 8.0,
     'L0_conv_fc1_w': 2.78}
    for name, (base, spread) in spreads.items():
        noise = np.random.default_rng([zlib.crc32(name.encode()), seed]).standard_normal(out[name].shape)
        drawn = base * np.exp(spread * noise) if base else spread * noise
        out[name] = jnp.asarray(drawn.astype(out[name].dtype))
    for name, factor in factors.items():
        out[name] = (out[name] * factor).astype(out[name].dtype)
    return out
```

```python
from contextlib import ExitStack

import numpy as np

import concourse.bass as bass
from concourse import mybir
from concourse.alu_op_type import AluOpType as ALU

F32 = mybir.dt.float32
F32R = mybir.dt.float32r
ACT = mybir.ActivationFunctionType
AX = mybir.AxisListType

IMAGES, H, W, C = 4, 128, 128, 48
WIN = 8
TOK = WIN * WIN
HEADS = 3
HD = C // HEADS
HID = 4 * C
SCALE = HD ** -0.5
EPS = 1e-5
STRIPES = IMAGES * H // WIN
BATCHES = STRIPES // 2
QUADS = 8
HALF = 4
C2 = 2 * C
ROW = 2 * WIN * C
REL = 2 * WIN - 1
TABLE = REL * REL
CHUNKS = 2 * HID // 128
MIX = 2 * 2 * HD + 2
GROUPS = 2 * WIN


def swin_block(nc, x, n1g, n1b, qkvw, qkvb, projw, projb, table, n2g, n2b, w1, b1, w2, b2, out):
    with ExitStack() as ctx:
        def sb(name, shape, dtype=F32):
            return ctx.enter_context(nc.sbuf_tensor(name, shape, dtype))

        def ps(name):
            return ctx.enter_context(nc.psum_tensor(name, [128, 512], F32))

        def sem(name):
            return ctx.enter_context(nc.semaphore(name))

        x_front = x.rearrange("m (s i) (a q bj) c -> (m s) q a i (bj c)", i=WIN, a=2, bj=2 * WIN)
        x_back = x.rearrange("m (s i) (a qb j) c -> (m s) a qb i (j c)", i=WIN, a=2, j=WIN)
        out_back = out.rearrange("m (s i) (a qb j) c -> (m s) a qb i (j c)", i=WIN, a=2, j=WIN)

        x2 = sb("x2", [128, BATCHES * ROW])
        x_in = sb("x_in", [128, ROW])
        stats = sb("stats", [128, GROUPS, 6])
        small = sb("small", [128, 8, GROUPS])
        rstd = sb("rstd", [128, GROUPS])
        minus_half = sb("minus_half", [128, GROUPS])
        fourth = sb("fourth", [128, GROUPS])
        centred = sb("centred", [128, GROUPS, C])
        normed = sb("normed", [128, WIN, C2])
        tokens_t = sb("tokens_t", [C2 + 1, QUADS, 2 * TOK])
        q_blocks = sb("q_blocks", [C2, 2, 2, TOK])
        k_blocks = sb("k_blocks", [C2, 2, HEADS, TOK])
        v_blocks = sb("v_blocks", [128, 2, HEADS, MIX])
        neg_max = sb("neg_max", [128, 2 * HEADS], F32R)
        probs = sb("probs", [128, HEADS, 2, TOK])
        probs_t = sb("probs_t", [128, HEADS, 128])
        inv_sum = sb("inv_sum", [128, HEADS, 2])
        heads = sb("heads", [128, 2, HEADS, HD])
        heads_t = sb("heads_t", [C2 + 1, WIN, QUADS * 2 * WIN])
        tokens2_t = sb("tokens2_t", [C2 + 1, 2, HALF * 128])
        hidden = sb("hidden", [128, 2, CHUNKS, HALF * 128])

        wqkv = sb("wqkv", [C2 + 1, 3 * C2])
        wqkv_in = sb("wqkv_in", [C2, 3 * C2])
        wproj = sb("wproj", [C2 + 1, C2])
        wfc1 = sb("wfc1", [C2 + 1, 2 * HID])
        wfc1_in = sb("wfc1_in", [C2, 2 * HID])
        wfc2 = sb("wfc2", [128, CHUNKS, C2])
        fc2_bias = sb("fc2_bias", [128, C])
        gains = sb("gains", [C2, 2])
        shifts = sb("shifts", [C2, 2, C2 + 1])
        bias_row = sb("bias_row", [C2 + 1, 3 * C2 + 2 * HID])
        pos_in = sb("pos_in", [128, HEADS, WIN, WIN])
        pos_high = sb("pos_high", [128, HEADS * TOK], F32R)
        pos = sb("pos", [128, 2, HEADS * TOK], F32R)
        ident = sb("ident", [128, 128])
        ident_r = sb("ident_r", [128, 128], F32R)
        flip = sb("flip", [128, 2, TOK])
        flip_r = sb("flip_r", [128, 2 * TOK], F32R)
        row_mask = sb("row_mask", [C2, HEADS, 2])
        q_mask = sb("q_mask", [C2, 2])

        turn_ps = ps("turn_ps")
        q_ps = ps("q_ps")
        kv_ps = ps("kv_ps")
        scores_ps = [ps("scores_ps0"), ps("scores_ps1")]
        probs_t_ps = ps("probs_t_ps")
        mixed_ps = ps("mixed_ps")
        heads_t_ps = ps("heads_t_ps")
        fc1_ps = [q_ps, kv_ps, probs_t_ps]
        fc2_ps = scores_ps

        zeroed = sem("zeroed")
        weights_in = sem("weights_in")
        weights_ok = sem("weights_ok")
        consts_made = sem("consts_made")
        pool_step = sem("pool_step")
        setup_dve = sem("setup_dve")
        blocks_zeroed = sem("blocks_zeroed")
        bias_mm = sem("bias_mm")
        x_loaded = sem("x_loaded")
        res_loaded = sem("res_loaded")
        stats_ok = sem("stats_ok")
        normed_ok = sem("normed_ok")
        small_step = sem("small_step")
        turned = sem("turned")
        tokens_t_ok = sem("tokens_t_ok")
        q_mm = sem("q_mm")
        kv_mm = sem("kv_mm")
        q_ok = sem("q_ok")
        k_ok = sem("k_ok")
        v_ok = sem("v_ok")
        scores_mm = sem("scores_mm")
        max_ok = sem("max_ok")
        less_max_mm = sem("less_max_mm")
        probs_ok = sem("probs_ok")
        probs_turned = sem("probs_turned")
        probs_t_ok = sem("probs_t_ok")
        mixed_mm = sem("mixed_mm")
        inv_ok = sem("inv_ok")
        heads_ok = sem("heads_ok")
        heads_turned = sem("heads_turned")
        heads_t_ok = sem("heads_t_ok")
        proj_mm = sem("proj_mm")
        x2_ok = sem("x2_ok")
        stats2_ok = sem("stats2_ok")
        normed2_ok = sem("normed2_ok")
        biased2_ok = sem("biased2_ok")
        small2_step = sem("small2_step")
        turned2 = sem("turned2")
        tokens2_t_ok = sem("tokens2_t_ok")
        fc1_mm = sem("fc1_mm")
        hidden_ok = sem("hidden_ok")
        fc2_mm = sem("fc2_mm")
        out_ok = sem("out_ok")
        stored = sem("stored")

        N_WEIGHT_DMAS = 81
        SMALL_STEPS = 10

        def wait(eng, semaphore, count):
            if not (isinstance(count, int) and count <= 0):
                eng.wait_ge(semaphore, count)

        def batches(eng, body):
            body(0, True, False)
            with eng.Fori(1, BATCHES - 1) as n:
                body(n, False, False)
            body(BATCHES - 1, False, True)

        def x2_batch(n):
            return x2[:, bass.ds(n * ROW, ROW)].rearrange("p (a j c) -> p a j c", a=2, j=WIN)

        def x2_half(n, half):
            return x2_batch(n)[:, :, HALF * half:HALF * half + HALF, :].rearrange("p a j c -> p j a c")

        def broadcast(ap, axis, count):
            shape = list(ap.shape)
            shape.insert(axis, count)
            return ap.unsqueeze(axis).to_broadcast(shape)

        block = ctx.enter_context(nc.Block())

        @block.sync
        def _(sp):
            def load_front(n):
                for k in range(QUADS):
                    sp.dma_start(x_in[2 * WIN * k:2 * WIN * k + 2 * WIN, :],
                                 x_front[2 * n + k // HALF, k % HALF]).then_inc(x_loaded, 16)

            load_front(0)
            sp.wait_ge(zeroed, 1)
            count = 0

            def load(dst, src):
                nonlocal count
                sp.dma_start(dst, src).then_inc(weights_in, 16)
                count += 1

            def row(v):
                return v.rearrange("(o n) -> o n", o=1)

            def column(v):
                return v.rearrange("(n o) -> n o", o=1)

            for half in range(2):
                for pi in range(WIN):
                    p = TOK * half + WIN * pi
                    for h in range(HEADS):
                        load(pos_in[p:p + WIN, h], bass.AP(
                            table.tensor, TABLE * h + REL * pi, [[1, WIN], [REL, WIN], [1, WIN]]))
            for b in range(2):
                rows = slice(C * b, C * b + C)
                for m in range(2):
                    dst = wqkv_in[rows, C2 * m:C2 * m + C2].rearrange("c (h b d) -> c h b d", h=HEADS, b=2)
                    load(dst[:, :, b, :], qkvw[:, C * m:C * m + C].rearrange("c (h d) -> c h d", h=HEADS))
                    dst = bias_row[C2:C2 + 1, C2 * m:C2 * m + C2].rearrange("c (h b d) -> c h b d", h=HEADS, b=2)
                    load(dst[:, :, b, :], row(qkvb)[:, C * m:C * m + C].rearrange("c (h d) -> c h d", h=HEADS))
                at = 2 * C2 + C * b
                load(wqkv_in[rows, at:at + C], qkvw[:, 2 * C:3 * C])
                load(bias_row[C2:C2 + 1, at:at + C], row(qkvb)[:, 2 * C:3 * C])
                load(wproj[rows, C * b:C * b + C], projw)
                load(wproj[C2:C2 + 1, C * b:C * b + C], row(projb))
                load(wfc1_in[rows, HID * b:HID * b + HID], w1)
                at = 3 * C2 + HID * b
                load(bias_row[C2:C2 + 1, at:at + HID], row(b1))
                for m, (gain, shift) in enumerate(((n1g, n1b), (n2g, n2b))):
                    load(gains[rows, m:m + 1], column(gain))
                    load(shifts[rows, m, C2:C2 + 1], column(shift))
                at = HID * b
                while at < HID * (b + 1):
                    end = min(HID * (b + 1), (at // 128 + 1) * 128)
                    load(wfc2[at % 128:at % 128 + end - at, at // 128, C * b:C * b + C],
                         w2[at - HID * b:end - HID * b, :])
                    at = end
            load(fc2_bias[:, :], row(b2).to_broadcast([128, C]))
            assert count == N_WEIGHT_DMAS, count

            def body(n, first, last):
                if not last:
                    wait(sp, normed_ok, n + 1)
                    load_front(n + 1)
                wait(sp, x2_ok, 2 * n)
                for s in range(2):
                    for a in range(2):
                        sp.dma_start(x2[64 * s:64 * s + 64, bass.ds(n * ROW + a * (ROW // 2), ROW // 2)],
                                     x_back[2 * n + s, a]).then_inc(res_loaded, 16)

            batches(sp, body)

            with sp.Fori(0, BATCHES) as n:
                sp.wait_ge(out_ok, 2 * n + 2)
                for s in range(2):
                    for a in range(2):
                        sp.dma_start(out_back[2 * n + s, a],
                                     x2[64 * s:64 * s + 64, bass.ds(n * ROW + a * (ROW // 2), ROW // 2)]
                                     ).then_inc(stored, 16)
            sp.wait_ge(stored, 64 * BATCHES)

        def layer_norm(pool, n, source, step, stats_sem):
            done = SMALL_STEPS * n
            mean_even, mean_odd, sq_even, sq_odd = (stats[:, :, f] for f in (1, 4, 2, 5))
            total, gap, squares, gap2, mean, scaled, quarter, variance = (small[:, f, :] for f in range(8))
            pool.wait_ge(stats_sem, n + 1)
            pool.tensor_tensor(total, mean_even, mean_odd, ALU.add).then_inc(step, 1)
            pool.tensor_tensor(gap, mean_even, mean_odd, ALU.subtract).then_inc(step, 1)
            pool.tensor_tensor(squares, sq_even, sq_odd, ALU.add).then_inc(step, 1)
            pool.wait_ge(step, done + 3)
            pool.tensor_tensor(gap2, gap, gap, ALU.mult).then_inc(step, 1)
            pool.tensor_scalar(mean, total, 0.5, None, ALU.mult).then_inc(step, 1)
            pool.tensor_scalar(scaled, squares, 1.0 / C, EPS, ALU.mult, ALU.add).then_inc(step, 1)
            pool.wait_ge(step, done + 6)
            pool.tensor_tensor(quarter, gap2, fourth[:, :], ALU.mult).then_inc(step, 1)
            pool.wait_ge(step, done + 7)
            pool.tensor_tensor(variance, scaled, quarter, ALU.add).then_inc(step, 1)
            pool.tensor_tensor(centred[:, :, :], source, broadcast(mean, 2, C), ALU.subtract).then_inc(step, 1)
            pool.wait_ge(step, done + 8)
            pool.tensor_tensor(rstd[:, :], variance, minus_half[:, :], ALU.pow).then_inc(step, 1)
            pool.wait_ge(step, done + 10)

        @block.gpsimd
        def _(pool):
            pool.memset(wqkv_in[:, :], 0.0)
            pool.memset(wfc1_in[:, :], 0.0)
            pool.memset(wfc2[:, :, :], 0.0)
            pool.memset(shifts[:, :, :], 0.0)
            pool.memset(wproj[:, :], 0.0).then_inc(zeroed, 1)
            pool.memset(ident[:, :], 0.0)
            pool.memset(flip[:, :, :], 0.0)
            pool.memset(minus_half[:, :], -0.5)
            pool.memset(fourth[:, :], 0.25)
            pool.memset(row_mask[:, :, :], SCALE).then_inc(pool_step, 1)
            pool.wait_ge(pool_step, 1)
            pool.affine_select(out=ident[:, :], in_=ident[:, :], compare_op=ALU.not_equal, fill=1.0,
                               base=0, pattern=[[-1, 128]], channel_multiplier=1)
            pool.affine_select(out=flip[:, :, :], in_=flip[:, :, :], compare_op=ALU.not_equal, fill=1.0,
                               base=1 - TOK, pattern=[[0, 2], [1, TOK]], channel_multiplier=1)
            pool.affine_select(out=row_mask[:, :, :], in_=row_mask[:, :, :], compare_op=ALU.is_ge, fill=0.0,
                               base=0, pattern=[[-2 * HD, HEADS], [-HD, 2]], channel_multiplier=1).then_inc(pool_step, 1)
            pool.wait_ge(pool_step, 2)
            pool.affine_select(out=flip[:, :, :], in_=flip[:, :, :], compare_op=ALU.not_equal, fill=1.0,
                               base=1 - 2 * TOK, pattern=[[0, 2], [1, TOK]], channel_multiplier=1)
            pool.affine_select(out=row_mask[:, :, :], in_=row_mask[:, :, :], compare_op=ALU.is_ge, fill=0.0,
                               base=HD - 1, pattern=[[2 * HD, HEADS], [HD, 2]], channel_multiplier=-1
                               ).then_inc(consts_made, 1)

            def norm_front(n):
                layer_norm(pool, n, x_in[:, :].rearrange("p (g c) -> p g c", c=C), small_step, stats_ok)
                wait(pool, turned, 2 * n)
                pool.tensor_tensor(
                    normed[:, :, :].rearrange("p j (b c) -> p b j c", b=2),
                    centred[:, :, :].rearrange("p (b j) c -> p b j c", b=2),
                    broadcast(rstd[:, :].rearrange("p (b j) -> p b j", b=2), 3, C),
                    ALU.mult).then_inc(normed_ok, 1)

            norm_front(0)
            with pool.Fori(1, BATCHES) as n:
                norm_front(n)

            def norm_back(n):
                layer_norm(pool, n, x2_batch(n).rearrange("p a j c -> p (a j) c"), small2_step, stats2_ok)
                if isinstance(n, int) and n == 0:
                    pool.wait_ge(turned, 2 * BATCHES)
                else:
                    pool.wait_ge(turned2, 2 * n)
                pool.tensor_tensor(
                    normed[:, :, :].rearrange("p j (a c) -> p a j c", a=2),
                    centred[:, :, :].rearrange("p (a j) c -> p a j c", a=2),
                    broadcast(rstd[:, :].rearrange("p (a j) -> p a j", a=2), 3, C),
                    ALU.mult).then_inc(normed2_ok, 1)
                residual = x2_batch(n).rearrange("p a j c -> p (a j) c")
                pool.tensor_tensor(residual, residual, broadcast(fc2_bias[:, :], 1, GROUPS),
                                   ALU.add).then_inc(biased2_ok, 1)

            norm_back(0)
            with pool.Fori(1, BATCHES) as n:
                norm_back(n)

        @block.tensor
        def _(pe):
            pe.wait_ge(weights_in, 16 * (N_WEIGHT_DMAS))
            pe.matmul(q_ps[0:C2 + 1, 0:3 * C2], shifts[:, 0, :], wqkv_in[:, :], start=True, stop=True)
            pe.matmul(kv_ps[0:C2 + 1, 0:2 * HID], shifts[:, 1, :], wfc1_in[:, :], start=True, stop=True).then_inc(bias_mm, 1)
            pe.wait_ge(weights_ok, 1)

            def turn_tokens(half, bank):
                for m in range(HALF):
                    mm = pe.transpose(bank[0:C2, 128 * m:128 * m + 128], normed[:, HALF * half + m, :], ident[:, :])
                mm.then_inc(turned, 1)

            def project_qkv(k):
                tokens = tokens_t[:, k, :]
                pe.matmul(q_ps[0:C2, 0:2 * TOK], wqkv[:, 0:C2], tokens, start=True, stop=True).then_inc(q_mm, 1)
                pe.matmul(kv_ps[0:C2, 0:2 * TOK], wqkv[:, C2:2 * C2], tokens, start=True, stop=True)
                pe.matmul(kv_ps[:, 128:128 + C2], tokens, wqkv[:, 2 * C2:3 * C2], start=True, stop=True).then_inc(kv_mm, 1)

            def scores(k):
                bank = scores_ps[k % 2]
                pe.matmul(bank[:, 0:2 * HEADS * TOK], flip_r[:, :], pos[:, :, :].rearrange("p a n -> p (a n)"),
                          start=True, stop=False, skip_group_check=True)
                for a in range(2):
                    at = HEADS * TOK * a
                    mm = pe.matmul(bank[:, at:at + HEADS * TOK], q_blocks[:, a, :, :].rearrange("p b q -> p (b q)"),
                                   k_blocks[:, a, :, :].rearrange("p h t -> p (h t)"),
                                   start=False, stop=False, skip_group_check=True)
                mm.then_inc(scores_mm, 1)

            def less_max(k):
                pe.matmul(scores_ps[k % 2][:, 0:2 * HEADS * TOK].rearrange("p (r t) -> p r t", t=TOK), ident_r[:, :],
                          broadcast(neg_max[:, :], 2, TOK),
                          start=False, stop=True, skip_group_check=True).then_inc(less_max_mm, 1)

            def turn_probs():
                for h in range(HEADS):
                    mm = pe.transpose(probs_t_ps[:, 128 * h:128 * h + 128],
                                      probs[:, h, :, :].rearrange("p a t -> p (a t)"), ident[:, :])
                mm.then_inc(probs_turned, 1)

            def mix(k):
                for h in range(HEADS):
                    mm = pe.matmul(mixed_ps[:, MIX * h:MIX * h + MIX], probs_t[:, h, :], v_blocks[:, k % 2, h, :],
                                   start=True, stop=True)
                mm.then_inc(mixed_mm, 1)

            def turn_heads():
                pe.transpose(heads_t_ps[0:C2, 0:128], heads[:, :, :, :].rearrange("p a h d -> p (a h d)"),
                             ident[:, :]).then_inc(heads_turned, 1)

            def project_heads(half):
                for m in range(HALF):
                    mm = pe.matmul(turn_ps[:, C2 * m:C2 * m + C2], heads_t[:, HALF * half + m, :], wproj[:, :],
                                   start=True, stop=True)
                mm.then_inc(proj_mm, 1)

            def body(n, first, last):
                g0 = QUADS * n
                for k in range(QUADS):
                    if k == 2 and not first:
                        wait(pe, heads_t_ok, g0)
                        project_heads(0)
                    wait(pe, q_ok, g0 + k + 1)
                    wait(pe, k_ok, g0 + k + 1)
                    wait(pe, probs_ok, g0 + k - 1)
                    scores(k)
                    if k == 2 and not first:
                        wait(pe, x2_ok, 2 * n - 1)
                        project_heads(1)
                    if not (first and k < 2):
                        wait(pe, heads_ok, g0 + k - 1)
                        wait(pe, heads_t_ok, g0 + k - 2)
                        if k == 7 and not last:
                            wait(pe, tokens_t_ok, 2 * n + 4)
                        turn_heads()
                    if not (last and k == QUADS - 1):
                        if k == QUADS - 1:
                            wait(pe, tokens_t_ok, 2 * n + 4)
                        wait(pe, v_ok, g0 + k + 1)
                        project_qkv((k + 1) % QUADS)
                    wait(pe, max_ok, g0 + k + 1)
                    less_max(k)
                    if not (first and k == 0):
                        wait(pe, probs_t_ok, g0 + k)
                        wait(pe, heads_ok, g0 + k - 1)
                        mix((k - 1) % 2)
                    wait(pe, probs_ok, g0 + k + 1)
                    turn_probs()
                    if k == 6 and not last:
                        wait(pe, normed_ok, n + 2)
                        wait(pe, x2_ok, 2 * n)
                        turn_tokens(0, turn_ps)
                        wait(pe, heads_t_ok, g0 + k - 1)
                        turn_tokens(1, heads_t_ps)

            pe.wait_ge(consts_made, 1)
            pe.wait_ge(normed_ok, 1)
            turn_tokens(0, turn_ps)
            turn_tokens(1, heads_t_ps)
            pe.wait_ge(tokens_t_ok, 2)
            project_qkv(0)
            batches(pe, body)
            total = QUADS * BATCHES
            pe.wait_ge(heads_ok, total - 1)
            pe.wait_ge(heads_t_ok, total - 2)
            turn_heads()
            pe.wait_ge(probs_t_ok, total)
            mix(1)
            pe.wait_ge(heads_ok, total)
            pe.wait_ge(heads_t_ok, total - 1)
            turn_heads()
            pe.wait_ge(heads_t_ok, total)
            project_heads(0)
            pe.wait_ge(x2_ok, 2 * BATCHES - 1)
            project_heads(1)

            def turn_tokens2(half):
                for m in range(HALF):
                    mm = pe.transpose(turn_ps[0:C2, 128 * m:128 * m + 128], normed[:, HALF * half + m, :], ident[:, :])
                mm.then_inc(turned2, 1)

            def fc1(r, half):
                for chunk in range(CHUNKS):
                    wait(pe, hidden_ok, CHUNKS * (r - 1) + chunk + 1)
                    pe.matmul(fc1_ps[chunk][:, :], wfc1[:, 128 * chunk:128 * chunk + 128], tokens2_t[:, half, :],
                              start=True, stop=True).then_inc(fc1_mm, 1)

            def fc2(half):
                for m in range(HALF):
                    for chunk in range(CHUNKS):
                        mm = pe.matmul(fc2_ps[half][:, C2 * m:C2 * m + C2],
                                       hidden[:, half, chunk, 128 * m:128 * m + 128], wfc2[:, chunk, :],
                                       start=(chunk == 0), stop=(chunk == CHUNKS - 1))
                mm.then_inc(fc2_mm, 1)

            def back(n, first, last):
                for half in range(2):
                    r = 2 * n + half
                    wait(pe, tokens2_t_ok, r + 1)
                    fc1(r, half)
                    if not (last and half == 1):
                        if half == 1:
                            wait(pe, normed2_ok, n + 2)
                        turn_tokens2(1 - half)
                    if not (first and half == 0):
                        wait(pe, hidden_ok, CHUNKS * r)
                        wait(pe, out_ok, r - 2)
                        fc2(1 - half)

            pe.wait_ge(x2_ok, 2 * BATCHES)
            pe.wait_ge(normed2_ok, 1)
            turn_tokens2(0)
            batches(pe, back)
            pe.wait_ge(hidden_ok, CHUNKS * 2 * BATCHES)
            pe.wait_ge(out_ok, 2 * BATCHES - 2)
            fc2(1)

        @block.scalar
        def _(act):
            def tokens_out(bank, half):
                act.activation(
                    tokens_t[0:C2, :, :].rearrange("c k (ai j) -> c j (k ai)", j=WIN)[:, HALF * half:HALF * half + HALF, :],
                    bank[0:C2, :].rearrange("c (j t) -> c j t", j=HALF), ACT.Copy).then_inc(tokens_t_ok, 1)

            def k_out():
                for h in range(HEADS):
                    rows = slice(2 * HD * h, 2 * HD * h + 2 * HD)
                    ins = act.activation(k_blocks[rows, :, h, :],
                                         kv_ps[rows, 0:2 * TOK].rearrange("p (a t) -> p a t", a=2), ACT.Copy)
                ins.then_inc(k_ok, 1)

            def v_out(k):
                for a in range(2):
                    rows = slice(TOK * a, TOK * a + TOK)
                    dst = v_blocks[rows, k % 2, :, 0:MIX - 2].rearrange("p h (b a d) -> p b h a d", b=2, a=2)
                    ins = act.activation(dst[:, :, :, a, :],
                                         kv_ps[rows, 128:128 + C2].rearrange("p (b h d) -> p b h d", b=2, h=HEADS), ACT.Copy)
                ins.then_inc(v_ok, 1)

            def exp(k):
                act.activation(probs[:, :, :, :].rearrange("p h a t -> p a h t"),
                               scores_ps[k % 2][:, 0:2 * HEADS * TOK].rearrange("p (a h t) -> p a h t", a=2, h=HEADS),
                               ACT.Exp).then_inc(probs_ok, 1)

            def heads_out(k):
                act.activation(heads_t[0:C2, :, 2 * WIN * k:2 * WIN * k + 2 * WIN],
                               heads_t_ps[0:C2, 0:128].rearrange("c (bi j) -> c j bi", j=WIN), ACT.Copy
                               ).then_inc(heads_t_ok, 1)

            def body(n, first, last):
                g0 = QUADS * n
                for k in range(QUADS):
                    if k == QUADS - 1 and not last:
                        wait(act, turned, 2 * n + 3)
                        wait(act, kv_mm, g0 + QUADS)
                        tokens_out(turn_ps, 0)
                        wait(act, turned, 2 * n + 4)
                        tokens_out(heads_t_ps, 1)
                    if not (first and k < 2):
                        wait(act, heads_turned, g0 + k - 1)
                        heads_out((k - 2) % QUADS)
                    if not (last and k == QUADS - 1):
                        wait(act, kv_mm, g0 + k + 2)
                        k_out()
                    wait(act, less_max_mm, g0 + k + 1)
                    exp(k)
                    if not (last and k == QUADS - 1):
                        wait(act, mixed_mm, g0 + k)
                        v_out(k + 1)

            act.wait_ge(consts_made, 1)
            act.wait_ge(turned, 1)
            tokens_out(turn_ps, 0)
            act.wait_ge(turned, 2)
            tokens_out(heads_t_ps, 1)
            act.wait_ge(blocks_zeroed, 1)
            act.wait_ge(kv_mm, 1)
            k_out()
            v_out(0)
            batches(act, body)
            total = QUADS * BATCHES
            for g in range(total - 2, total):
                act.wait_ge(heads_turned, g + 1)
                heads_out(g % QUADS)

            with act.Fori(0, BATCHES) as n:
                for half in range(2):
                    for chunk in range(CHUNKS):
                        act.wait_ge(fc1_mm, CHUNKS * (2 * n + half) + chunk + 1)
                        act.activation(hidden[:, half, chunk, :], fc1_ps[chunk][:, :], ACT.Gelu).then_inc(hidden_ok, 1)

        @block.vector
        def _(dve):
            dve.memset(tokens_t[C2:C2 + 1, :, :], 1.0)
            dve.memset(tokens2_t[C2:C2 + 1, :, :], 1.0)
            dve.memset(heads_t[C2:C2 + 1, :, :], 1.0)
            dve.memset(k_blocks[:, :, :, :], 0.0)
            dve.memset(v_blocks[:, :, :, :], 0.0).then_inc(setup_dve, 1)
            dve.wait_ge(setup_dve, 1)
            for a in range(2):
                ins = dve.memset(v_blocks[TOK * a:TOK * a + TOK, :, :, MIX - 2 + a:MIX - 1 + a], 1.0)
            ins.then_inc(blocks_zeroed, 1)
            dve.wait_ge(consts_made, 1)
            dve.tensor_reduce(q_mask[:, :], row_mask[:, :, :].rearrange("p h b -> p b h"), AX.X, ALU.add)
            dve.tensor_copy(ident_r[:, :], ident[:, :])
            dve.tensor_copy(flip_r[:, :], flip[:, :, :].rearrange("p b q -> p (b q)"))
            dve.wait_ge(weights_in, 16 * (N_WEIGHT_DMAS))
            pos_flat = pos_in[:, :, :, :].rearrange("p h i j -> p (h i j)")
            dve.tensor_scalar(wqkv[0:C2, :], wqkv_in[:, :], gains[:, 0:1], None, ALU.mult)
            dve.tensor_scalar(wfc1[0:C2, :], wfc1_in[:, :], gains[:, 1:2], None, ALU.mult)
            dve.tensor_copy(pos_high[:, :], pos_flat).then_inc(setup_dve, 1)
            dve.wait_ge(bias_mm, 1)
            dve.tensor_tensor(wqkv[C2:C2 + 1, :], q_ps[C2:C2 + 1, 0:3 * C2], bias_row[C2:C2 + 1, 0:3 * C2], ALU.add)
            dve.tensor_tensor(wfc1[C2:C2 + 1, :], kv_ps[C2:C2 + 1, 0:2 * HID],
                              bias_row[C2:C2 + 1, 3 * C2:3 * C2 + 2 * HID], ALU.add)
            dve.wait_ge(setup_dve, 2)
            for a in range(2):
                dve.tensor_copy(pos[0:TOK, a, :], pos_high[0:TOK, :].bitcast(F32))
                ins = dve.tensor_tensor(pos[TOK:2 * TOK, a, :], pos_flat[TOK:2 * TOK, :],
                                        pos_high[TOK:2 * TOK, :].bitcast(F32), ALU.subtract)
            ins.then_inc(weights_ok, 1)

            def take_stats(source, groups):
                for group in groups:
                    ins = dve.bn_stats(stats[:, group, :], source[:, group, :])
                return ins

            x_groups = x_in[:, :].rearrange("p (g c) -> p g c", c=C)

            def q_out():
                dve.tensor_tensor(
                    q_blocks[:, :, :, :],
                    broadcast(q_ps[0:C2, 0:2 * TOK].rearrange("p (a q) -> p a q", a=2), 2, 2),
                    broadcast(broadcast(q_mask[:, :], 1, 2), 3, TOK), ALU.mult).then_inc(q_ok, 1)

            def row_max(k):
                dve.tensor_reduce(neg_max[:, :], scores_ps[k % 2][:, 0:2 * HEADS * TOK].rearrange("p (r t) -> p r t", t=TOK),
                                  AX.X, ALU.max, negate=True).then_inc(max_ok, 1)

            def probs_t_out():
                dve.tensor_copy(probs_t[:, :, :], probs_t_ps[:, 0:HEADS * 128].rearrange("p (h q) -> p h q", h=HEADS)
                                ).then_inc(probs_t_ok, 1)

            def normalise(g):
                mixed = mixed_ps[:, 0:HEADS * MIX].rearrange("p (h m) -> p h m", h=HEADS)
                dve.reciprocal(inv_sum[:, :, :], mixed[:, :, MIX - 2:MIX]).then_inc(inv_ok, 1)
                dve.wait_ge(inv_ok, g + 1)
                for b in range(2):
                    rows = slice(TOK * b, TOK * b + TOK)
                    own = mixed[rows, :, 2 * HD * b:2 * HD * b + 2 * HD].rearrange("p h (a d) -> p h a d", a=2)
                    ins = dve.tensor_tensor(heads[rows, :, :, :].rearrange("p a h d -> p h a d"), own,
                                            broadcast(inv_sum[rows, :, :], 3, HD), ALU.mult)
                ins.then_inc(heads_ok, 1)

            def add_proj(n, half):
                tokens = x2_half(n, half)
                dve.tensor_tensor(tokens, turn_ps[:, 0:HALF * C2].rearrange("p (j a c) -> p j a c", j=HALF, a=2),
                                  tokens, ALU.add).then_inc(x2_ok, 1)

            def body(n, first, last):
                g0 = QUADS * n
                for k in range(QUADS):
                    if k == 2 and not first:
                        dve.wait_ge(res_loaded, 64 * n)
                        dve.wait_ge(proj_mm, 2 * n - 1)
                        add_proj(n - 1, 0)
                    wait(dve, scores_mm, g0 + k + 1)
                    row_max(k)
                    if not (last and k == QUADS - 1):
                        wait(dve, q_mm, g0 + k + 2)
                        q_out()
                    if k == 2 and not first:
                        dve.wait_ge(proj_mm, 2 * n)
                        add_proj(n - 1, 1)
                    if not (first and k == 0):
                        wait(dve, mixed_mm, g0 + k)
                        normalise(g0 + k - 1)
                    wait(dve, probs_turned, g0 + k + 1)
                    probs_t_out()
                    if not last:
                        if k == 0:
                            dve.wait_ge(normed_ok, n + 1)
                            dve.wait_ge(x_loaded, 16 * QUADS * (n + 2))
                        if k < 4:
                            ins = take_stats(x_groups, range(4 * k, 4 * k + 4))
                            if k == 3:
                                ins.then_inc(stats_ok, 1)

            dve.wait_ge(x_loaded, 16 * QUADS)
            take_stats(x_groups, range(GROUPS)).then_inc(stats_ok, 1)
            dve.wait_ge(q_mm, 1)
            q_out()
            batches(dve, body)
            total = QUADS * BATCHES
            dve.wait_ge(mixed_mm, total)
            normalise(total - 1)
            dve.wait_ge(res_loaded, 64 * BATCHES)
            for half in range(2):
                dve.wait_ge(proj_mm, 2 * BATCHES - 1 + half)
                add_proj(BATCHES - 1, half)

            def tokens2_out(half):
                dve.tensor_copy(tokens2_t[0:C2, half, :], turn_ps[0:C2, :]).then_inc(tokens2_t_ok, 1)

            def add_mlp(n, half):
                tokens = x2_half(n, half)
                dve.tensor_tensor(tokens, fc2_ps[half][:, 0:HALF * C2].rearrange("p (j a c) -> p j a c", j=HALF, a=2),
                                  tokens, ALU.add).then_inc(out_ok, 1)

            def stats_back(n, part):
                return take_stats(x2_batch(n).rearrange("p a j c -> p (a j) c"), range(8 * part, 8 * part + 8))

            def back(n, first, last):
                for half in range(2):
                    r = 2 * n + half
                    if not last:
                        if half == 0:
                            dve.wait_ge(normed2_ok, n + 1)
                        ins = stats_back(n + 1, half)
                        if half == 1:
                            ins.then_inc(stats2_ok, 1)
                    if not (last and half == 1):
                        dve.wait_ge(turned2, r + 2)
                        tokens2_out(1 - half)
                    if not (first and half == 0):
                        if half == 1:
                            dve.wait_ge(biased2_ok, n + 1)
                        dve.wait_ge(fc2_mm, r)
                        add_mlp(n if half else n - 1, 1 - half)

            dve.wait_ge(x2_ok, 2 * BATCHES)
            stats_back(0, 0)
            stats_back(0, 1).then_inc(stats2_ok, 1)
            dve.wait_ge(turned2, 1)
            tokens2_out(0)
            batches(dve, back)
            dve.wait_ge(fc2_mm, 2 * BATCHES)
            add_mlp(BATCHES - 1, 1)


_P = "L0_conv_"
_INS = ["x"] + [_P + n for n in ("norm1_g", "norm1_b", "qkv_w", "qkv_b", "proj_w", "proj_b", "rel_bias_table",
                                 "norm2_g", "norm2_b", "fc1_w", "fc1_b", "fc2_w", "fc2_b")]


def kernel(**inputs):
    import concourse.bacc as bacc
    from concourse.bass_utils import run_bass_kernel_spmd

    nc = bacc.Bacc("TRN2", target_bir_lowering=False, num_devices=1)
    arrays, args = {}, []
    for name in _INS:
        a = np.asarray(inputs[name])
        if name.endswith("rel_bias_table"):
            a = a[::-1].T
        a = np.ascontiguousarray(a)
        arrays[f"in_{name}"] = a
        args.append(nc.dram_tensor(f"in_{name}", a.shape, mybir.dt.from_np(a.dtype), kind="ExternalInput").ap())
    args.append(nc.dram_tensor("out", (IMAGES, H, W, C), F32, kind="ExternalOutput").ap())
    swin_block(nc, *args)
    r = run_bass_kernel_spmd(nc, [arrays], core_ids=[0])
    return r.results[0]["out"]
```

```python
from contextlib import ExitStack

import numpy as np

import concourse.bass as bass
from concourse import mybir
from concourse.alu_op_type import AluOpType as ALU

F32 = mybir.dt.float32
F32R = mybir.dt.float32r
ACT = mybir.ActivationFunctionType
AX = mybir.AxisListType

IMAGES, H, W, C = 4, 128, 128, 48
WIN = 8
TOK = WIN * WIN
HEADS = 3
HD = C // HEADS
HID = 4 * C
SCALE = HD ** -0.5
EPS = 1e-5
STRIPES = IMAGES * H // WIN
BATCHES = STRIPES // 2
QUADS = 8
HALF = 4
C2 = 2 * C
ROW = 2 * WIN * C
REL = 2 * WIN - 1
TABLE = REL * REL
CHUNKS = 2 * HID // 128
MIX = 2 * 2 * HD + 2
V_BUFS = 4
HIGH, LOW = 0, 1
PARTS = ((HIGH, LOW), (LOW, HIGH), (HIGH, HIGH))
GROUPS = 2 * WIN


def swin_block(nc, x, n1g, n1b, qkvw, qkvb, projw, projb, table, n2g, n2b, w1, b1, w2, b2, out):
    with ExitStack() as ctx:
        def sb(name, shape, dtype=F32):
            return ctx.enter_context(nc.sbuf_tensor(name, shape, dtype))

        def ps(name):
            return ctx.enter_context(nc.psum_tensor(name, [128, 512], F32))

        def sem(name):
            return ctx.enter_context(nc.semaphore(name))

        x_front = x.rearrange("m (s i) (a q bj) c -> (m s) q a i (bj c)", i=WIN, a=2, bj=2 * WIN)
        x_back = x.rearrange("m (s i) (a qb j) c -> (m s) a qb i (j c)", i=WIN, a=2, j=WIN)
        out_back = out.rearrange("m (s i) (a qb j) c -> (m s) a qb i (j c)", i=WIN, a=2, j=WIN)

        x2 = sb("x2", [128, BATCHES * ROW])
        x_in = sb("x_in", [128, ROW])
        stats = sb("stats", [128, GROUPS, 6])
        small = sb("small", [128, 8, GROUPS])
        rstd = sb("rstd", [128, GROUPS])
        minus_half = sb("minus_half", [128, GROUPS])
        fourth = sb("fourth", [128, GROUPS])
        centred = sb("centred", [128, GROUPS, C])
        normed = sb("normed", [128, WIN, C2])
        tokens_t = sb("tokens_t", [C2 + 1, QUADS, 2 * TOK])
        q_blocks = sb("q_blocks", [C2, 2, 2, TOK])
        k_blocks = sb("k_blocks", [C2, 2, HEADS, TOK])
        v_blocks = sb("v_blocks", [128, V_BUFS, HEADS, MIX])
        neg_max = sb("neg_max", [128, 2 * HEADS], F32R)
        probs = sb("probs", [128, HEADS, 2, TOK])
        probs_t = sb("probs_t", [128, HEADS, 128])
        inv_sum = sb("inv_sum", [128, HEADS, 2])
        heads = sb("heads", [128, 2, 2, HEADS, HD])
        heads_t = sb("heads_t", [C2 + 1, WIN, QUADS * 2 * WIN])
        tokens2_t = sb("tokens2_t", [C2 + 1, 2, 2, HALF * 128], F32R)
        hidden = sb("hidden", [128, 2, CHUNKS, HALF * 128])

        wqkv = sb("wqkv", [C2 + 1, 3 * C2])
        wqkv_in = sb("wqkv_in", [C2, 3 * C2])
        wproj = sb("wproj", [C2 + 1, C2])
        wfc1 = sb("wfc1", [C2 + 1, 2 * HID])
        wfc1_in = sb("wfc1_in", [C2, 2 * HID])
        wfc1_r = sb("wfc1_r", [C2 + 1, 2, 2 * HID], F32R)
        wfc2 = sb("wfc2", [128, CHUNKS, C2])
        fc2_bias = sb("fc2_bias", [128, C])
        gains = sb("gains", [C2, 2])
        shifts = sb("shifts", [C2, 2, C2 + 1])
        bias_row = sb("bias_row", [C2 + 1, 3 * C2 + 2 * HID])
        pos_in = sb("pos_in", [128, HEADS, WIN, WIN])
        pos_high = sb("pos_high", [128, HEADS * TOK], F32R)
        pos = sb("pos", [128, 2, HEADS * TOK], F32R)
        ident = sb("ident", [128, 128])
        ident_r = sb("ident_r", [128, 128], F32R)
        flip = sb("flip", [128, 2, TOK])
        flip_r = sb("flip_r", [128, 2 * TOK], F32R)
        row_mask = sb("row_mask", [C2, HEADS, 2])
        q_mask = sb("q_mask", [C2, 2])

        turn_ps = ps("turn_ps")
        q_ps = ps("q_ps")
        kv_ps = ps("kv_ps")
        scores_ps = [ps("scores_ps0"), ps("scores_ps1")]
        probs_t_ps = ps("probs_t_ps")
        mixed_ps = ps("mixed_ps")
        heads_t_ps = ps("heads_t_ps")
        fc1_ps = [q_ps, kv_ps, probs_t_ps]
        fc2_ps = scores_ps

        zeroed = sem("zeroed")
        weights_in = sem("weights_in")
        weights_ok = sem("weights_ok")
        consts_made = sem("consts_made")
        pool_step = sem("pool_step")
        setup_dve = sem("setup_dve")
        blocks_zeroed = sem("blocks_zeroed")
        bias_mm = sem("bias_mm")
        x_loaded = sem("x_loaded")
        res_loaded = sem("res_loaded")
        stats_ok = sem("stats_ok")
        normed_ok = sem("normed_ok")
        small_step = sem("small_step")
        turned = sem("turned")
        tokens_t_ok = sem("tokens_t_ok")
        q_mm = sem("q_mm")
        kv_mm = sem("kv_mm")
        q_ok = sem("q_ok")
        k_ok = sem("k_ok")
        v_ok = sem("v_ok")
        scores_mm = sem("scores_mm")
        max_ok = sem("max_ok")
        less_max_mm = sem("less_max_mm")
        probs_ok = sem("probs_ok")
        probs_turned = sem("probs_turned")
        probs_t_ok = sem("probs_t_ok")
        mixed_mm = sem("mixed_mm")
        inv_ok = sem("inv_ok")
        heads_ok = sem("heads_ok")
        heads_turned = sem("heads_turned")
        heads_t_ok = sem("heads_t_ok")
        proj_mm = sem("proj_mm")
        x2_ok = sem("x2_ok")
        stats2_ok = sem("stats2_ok")
        normed2_ok = sem("normed2_ok")
        biased2_ok = sem("biased2_ok")
        small2_step = sem("small2_step")
        turned2 = sem("turned2")
        tokens2_high = sem("tokens2_high")
        tokens2_t_ok = sem("tokens2_t_ok")
        fc1_mm = sem("fc1_mm")
        hidden_ok = sem("hidden_ok")
        fc2_mm = sem("fc2_mm")
        out_ok = sem("out_ok")
        stored = sem("stored")

        N_WEIGHT_DMAS = 81
        SMALL_STEPS = 10

        def wait(eng, semaphore, count):
            if not (isinstance(count, int) and count <= 0):
                eng.wait_ge(semaphore, count)

        def batches(eng, body):
            body(0, True, False)
            with eng.Fori(1, BATCHES - 1) as n:
                body(n, False, False)
            body(BATCHES - 1, False, True)

        def x2_batch(n):
            return x2[:, bass.ds(n * ROW, ROW)].rearrange("p (a j c) -> p a j c", a=2, j=WIN)

        def x2_half(n, half):
            return x2_batch(n)[:, :, HALF * half:HALF * half + HALF, :].rearrange("p a j c -> p j a c")

        def broadcast(ap, axis, count):
            shape = list(ap.shape)
            shape.insert(axis, count)
            return ap.unsqueeze(axis).to_broadcast(shape)

        def token_view(half):
            view = tokens_t[0:C2, :, :].rearrange("c k (ai j) -> c j (k ai)", j=WIN)
            return view[:, HALF * half:HALF * half + HALF, :]

        block = ctx.enter_context(nc.Block())

        @block.sync
        def _(sp):
            def load_front(n):
                for k in range(QUADS):
                    sp.dma_start(x_in[2 * WIN * k:2 * WIN * k + 2 * WIN, :],
                                 x_front[2 * n + k // HALF, k % HALF]).then_inc(x_loaded, 16)

            load_front(0)
            sp.wait_ge(zeroed, 1)
            count = 0

            def load(dst, src):
                nonlocal count
                sp.dma_start(dst, src).then_inc(weights_in, 16)
                count += 1

            def row(v):
                return v.rearrange("(o n) -> o n", o=1)

            def column(v):
                return v.rearrange("(n o) -> n o", o=1)

            for half in range(2):
                for pi in range(WIN):
                    p = TOK * half + WIN * pi
                    for h in range(HEADS):
                        load(pos_in[p:p + WIN, h], bass.AP(
                            table.tensor, TABLE * h + REL * pi, [[1, WIN], [REL, WIN], [1, WIN]]))
            for b in range(2):
                rows = slice(C * b, C * b + C)
                for m in range(2):
                    dst = wqkv_in[rows, C2 * m:C2 * m + C2].rearrange("c (h b d) -> c h b d", h=HEADS, b=2)
                    load(dst[:, :, b, :], qkvw[:, C * m:C * m + C].rearrange("c (h d) -> c h d", h=HEADS))
                    dst = bias_row[C2:C2 + 1, C2 * m:C2 * m + C2].rearrange("c (h b d) -> c h b d", h=HEADS, b=2)
                    load(dst[:, :, b, :], row(qkvb)[:, C * m:C * m + C].rearrange("c (h d) -> c h d", h=HEADS))
                at = 2 * C2 + C * b
                load(wqkv_in[rows, at:at + C], qkvw[:, 2 * C:3 * C])
                load(bias_row[C2:C2 + 1, at:at + C], row(qkvb)[:, 2 * C:3 * C])
                load(wproj[rows, C * b:C * b + C], projw)
                load(wproj[C2:C2 + 1, C * b:C * b + C], row(projb))
                load(wfc1_in[rows, HID * b:HID * b + HID], w1)
                at = 3 * C2 + HID * b
                load(bias_row[C2:C2 + 1, at:at + HID], row(b1))
                for m, (gain, shift) in enumerate(((n1g, n1b), (n2g, n2b))):
                    load(gains[rows, m:m + 1], column(gain))
                    load(shifts[rows, m, C2:C2 + 1], column(shift))
                at = HID * b
                while at < HID * (b + 1):
                    end = min(HID * (b + 1), (at // 128 + 1) * 128)
                    load(wfc2[at % 128:at % 128 + end - at, at // 128, C * b:C * b + C],
                         w2[at - HID * b:end - HID * b, :])
                    at = end
            load(fc2_bias[:, :], row(b2).to_broadcast([128, C]))
            assert count == N_WEIGHT_DMAS, count

            def body(n, first, last):
                if not last:
                    wait(sp, normed_ok, 2 * n + 2)
                    load_front(n + 1)
                wait(sp, x2_ok, 2 * n)
                for s in range(2):
                    for a in range(2):
                        sp.dma_start(x2[64 * s:64 * s + 64, bass.ds(n * ROW + a * (ROW // 2), ROW // 2)],
                                     x_back[2 * n + s, a]).then_inc(res_loaded, 16)

            batches(sp, body)

            with sp.Fori(0, BATCHES) as n:
                sp.wait_ge(out_ok, 2 * n + 2)
                for s in range(2):
                    for a in range(2):
                        sp.dma_start(out_back[2 * n + s, a],
                                     x2[64 * s:64 * s + 64, bass.ds(n * ROW + a * (ROW // 2), ROW // 2)]
                                     ).then_inc(stored, 16)
            sp.wait_ge(stored, 64 * BATCHES)

        def layer_norm(pool, n, source, step, stats_sem):
            done = SMALL_STEPS * n
            mean_even, mean_odd, sq_even, sq_odd = (stats[:, :, f] for f in (1, 4, 2, 5))
            total, gap, squares, gap2, mean, scaled, quarter, variance = (small[:, f, :] for f in range(8))
            pool.wait_ge(stats_sem, n + 1)
            pool.tensor_tensor(total, mean_even, mean_odd, ALU.add).then_inc(step, 1)
            pool.tensor_tensor(gap, mean_even, mean_odd, ALU.subtract).then_inc(step, 1)
            pool.tensor_tensor(squares, sq_even, sq_odd, ALU.add).then_inc(step, 1)
            pool.wait_ge(step, done + 3)
            pool.tensor_tensor(gap2, gap, gap, ALU.mult).then_inc(step, 1)
            pool.tensor_scalar(mean, total, 0.5, None, ALU.mult).then_inc(step, 1)
            pool.tensor_scalar(scaled, squares, 1.0 / C, EPS, ALU.mult, ALU.add).then_inc(step, 1)
            pool.wait_ge(step, done + 6)
            pool.tensor_tensor(quarter, gap2, fourth[:, :], ALU.mult).then_inc(step, 1)
            pool.wait_ge(step, done + 7)
            pool.tensor_tensor(variance, scaled, quarter, ALU.add).then_inc(step, 1)
            pool.tensor_tensor(centred[:, :, :], source, broadcast(mean, 2, C), ALU.subtract).then_inc(step, 1)
            pool.wait_ge(step, done + 8)
            pool.tensor_tensor(rstd[:, :], variance, minus_half[:, :], ALU.pow).then_inc(step, 1)
            pool.wait_ge(step, done + 10)

        def scale_half(pool, half):
            js = slice(HALF * half, HALF * half + HALF)
            return pool.tensor_tensor(
                normed[:, js, :].rearrange("p j (w c) -> p w j c", w=2),
                centred[:, :, :].rearrange("p (w j) c -> p w j c", w=2)[:, :, js, :],
                broadcast(rstd[:, :].rearrange("p (w j) -> p w j", w=2)[:, :, js], 3, C), ALU.mult)

        @block.gpsimd
        def _(pool):
            pool.memset(wqkv_in[:, :], 0.0)
            pool.memset(wfc1_in[:, :], 0.0)
            pool.memset(wfc2[:, :, :], 0.0)
            pool.memset(shifts[:, :, :], 0.0)
            pool.memset(wproj[:, :], 0.0).then_inc(zeroed, 1)
            pool.memset(ident[:, :], 0.0)
            pool.memset(flip[:, :, :], 0.0)
            pool.memset(minus_half[:, :], -0.5)
            pool.memset(fourth[:, :], 0.25)
            pool.memset(row_mask[:, :, :], SCALE).then_inc(pool_step, 1)
            pool.wait_ge(pool_step, 1)
            pool.affine_select(out=ident[:, :], in_=ident[:, :], compare_op=ALU.not_equal, fill=1.0,
                               base=0, pattern=[[-1, 128]], channel_multiplier=1)
            pool.affine_select(out=flip[:, :, :], in_=flip[:, :, :], compare_op=ALU.not_equal, fill=1.0,
                               base=1 - TOK, pattern=[[0, 2], [1, TOK]], channel_multiplier=1)
            pool.affine_select(out=row_mask[:, :, :], in_=row_mask[:, :, :], compare_op=ALU.is_ge, fill=0.0,
                               base=0, pattern=[[-2 * HD, HEADS], [-HD, 2]], channel_multiplier=1).then_inc(pool_step, 1)
            pool.wait_ge(pool_step, 2)
            pool.affine_select(out=flip[:, :, :], in_=flip[:, :, :], compare_op=ALU.not_equal, fill=1.0,
                               base=1 - 2 * TOK, pattern=[[0, 2], [1, TOK]], channel_multiplier=1)
            pool.affine_select(out=row_mask[:, :, :], in_=row_mask[:, :, :], compare_op=ALU.is_ge, fill=0.0,
                               base=HD - 1, pattern=[[2 * HD, HEADS], [HD, 2]], channel_multiplier=-1
                               ).then_inc(consts_made, 1)

            def norm_front(n):
                layer_norm(pool, n, x_in[:, :].rearrange("p (g c) -> p g c", c=C), small_step, stats_ok)
                for half in range(2):
                    wait(pool, turned, 2 * n - 1 + half)
                    scale_half(pool, half).then_inc(normed_ok, 1)

            norm_front(0)
            with pool.Fori(1, BATCHES) as n:
                norm_front(n)

            def norm_back(n):
                layer_norm(pool, n, x2_batch(n).rearrange("p a j c -> p (a j) c"), small2_step, stats2_ok)
                for half in range(2):
                    if isinstance(n, int) and n == 0:
                        pool.wait_ge(turned, 2 * BATCHES - 1 + half)
                    else:
                        pool.wait_ge(turned2, 2 * n - 1 + half)
                    scale_half(pool, half).then_inc(normed2_ok, 1)

            norm_back(0)
            with pool.Fori(1, BATCHES) as n:
                norm_back(n)

        @block.tensor
        def _(pe):
            def turn_tokens(half, bank):
                for m in range(HALF):
                    mm = pe.transpose(bank[0:C2, 128 * m:128 * m + 128], normed[:, HALF * half + m, :], ident[:, :])
                mm.then_inc(turned, 1)

            def product(out, left, right):
                for i, (p, q) in enumerate(PARTS):
                    mm = pe.matmul(out, left(p), right(q), start=(i == 0), stop=(i == len(PARTS) - 1))
                return mm

            def project_qkv(k):
                tokens = tokens_t[:, k, :]

                def weights(m):
                    return wqkv[:, C2 * m:C2 * m + C2]

                pe.matmul(kv_ps[0:C2, 0:2 * TOK], weights(1), tokens, start=True, stop=True)
                pe.matmul(kv_ps[:, 128:128 + C2], tokens, weights(2), start=True, stop=True).then_inc(kv_mm, 1)
                pe.matmul(q_ps[0:C2, 0:2 * TOK], weights(0), tokens, start=True, stop=True).then_inc(q_mm, 1)

            def scores(k):
                bank = scores_ps[k % 2]
                pe.matmul(bank[:, 0:2 * HEADS * TOK], flip_r[:, :], pos[:, :, :].rearrange("p a n -> p (a n)"),
                          start=True, stop=False, skip_group_check=True)
                for a in range(2):
                    at = HEADS * TOK * a
                    mm = pe.matmul(bank[:, at:at + HEADS * TOK], q_blocks[:, a, :, :].rearrange("p b q -> p (b q)"),
                                   k_blocks[:, a, :, :].rearrange("p h t -> p (h t)"),
                                   start=False, stop=False, skip_group_check=True)
                mm.then_inc(scores_mm, 1)

            def less_max(k):
                pe.matmul(scores_ps[k % 2][:, 0:2 * HEADS * TOK].rearrange("p (r t) -> p r t", t=TOK), ident_r[:, :],
                          broadcast(neg_max[:, :], 2, TOK),
                          start=False, stop=True, skip_group_check=True).then_inc(less_max_mm, 1)

            def turn_probs():
                for h in range(HEADS):
                    mm = pe.transpose(probs_t_ps[:, 128 * h:128 * h + 128],
                                      probs[:, h, :, :].rearrange("p a t -> p (a t)"), ident[:, :])
                mm.then_inc(probs_turned, 1)

            def mix(k):
                for h in range(HEADS):
                    mm = pe.matmul(mixed_ps[:, MIX * h:MIX * h + MIX], probs_t[:, h, :], v_blocks[:, k % V_BUFS, h, :],
                                   start=True, stop=True)
                mm.then_inc(mixed_mm, 1)

            def turn_heads(k):
                pe.transpose(heads_t_ps[0:C2, 0:128], heads[:, k % 2, :, :, :].rearrange("p a h d -> p (a h d)"),
                             ident[:, :]).then_inc(heads_turned, 1)

            def project_heads(half):
                for m in range(HALF):
                    mm = pe.matmul(turn_ps[:, C2 * m:C2 * m + C2], heads_t[:, HALF * half + m, :], wproj[:, :],
                                   start=True, stop=True)
                mm.then_inc(proj_mm, 1)

            def turn_heads_of(g, k):
                wait(pe, heads_ok, g + 1)
                wait(pe, heads_t_ok, g)
                turn_heads(k)

            def body(n, first, last):
                g0 = QUADS * n
                for k in range(QUADS):
                    wait(pe, q_ok, g0 + k + 1)
                    wait(pe, k_ok, g0 + k + 1)
                    wait(pe, probs_ok, g0 + k - 1)
                    scores(k)
                    if k == 2 and not first:
                        wait(pe, heads_t_ok, g0)
                        project_heads(0)
                    if k == 6 and not last:
                        wait(pe, normed_ok, 2 * n + 4)
                        wait(pe, x2_ok, 2 * n)
                        turn_tokens(0, turn_ps)
                        wait(pe, heads_t_ok, g0 + k - 2)
                        turn_tokens(1, heads_t_ps)
                    if not (first and k == 0):
                        wait(pe, probs_ok, g0 + k)
                        wait(pe, probs_t_ok, g0 + k - 1)
                        turn_probs()
                    if k == 7 and not last:
                        wait(pe, tokens_t_ok, 2 * n + 4)
                        turn_heads_of(g0 + k - 3, k - 3)
                    if not (last and k == QUADS - 1):
                        wait(pe, v_ok, g0 + k + 1)
                        project_qkv((k + 1) % QUADS)
                    if k == 2 and not first:
                        wait(pe, x2_ok, 2 * n - 1)
                        project_heads(1)
                    wait(pe, max_ok, g0 + k + 1)
                    less_max(k)
                    if not (first and k < 2) and not (k == 6 and not last):
                        turn_heads_of(g0 + k - 2, k - 2)
                    if not (first and k == 0):
                        wait(pe, probs_t_ok, g0 + k)
                        wait(pe, heads_ok, g0 + k - 1)
                        mix(k - 1)

            pe.wait_ge(consts_made, 1)
            pe.wait_ge(normed_ok, 2)
            turn_tokens(0, turn_ps)
            turn_tokens(1, heads_t_ps)
            pe.wait_ge(weights_in, 16 * (N_WEIGHT_DMAS))
            pe.matmul(q_ps[0:C2 + 1, 0:3 * C2], shifts[:, 0, :], wqkv_in[:, :], start=True, stop=True)
            pe.matmul(kv_ps[0:C2 + 1, 0:2 * HID], shifts[:, 1, :], wfc1_in[:, :], start=True, stop=True).then_inc(bias_mm, 1)
            pe.wait_ge(weights_ok, 1)
            pe.wait_ge(tokens_t_ok, 2)
            project_qkv(0)
            batches(pe, body)
            total = QUADS * BATCHES
            pe.wait_ge(probs_ok, total)
            pe.wait_ge(probs_t_ok, total - 1)
            turn_probs()
            turn_heads_of(total - 2, QUADS - 2)
            pe.wait_ge(probs_t_ok, total)
            mix(QUADS - 1)
            turn_heads_of(total - 1, QUADS - 1)
            pe.wait_ge(heads_t_ok, total)
            project_heads(0)
            pe.wait_ge(x2_ok, 2 * BATCHES - 1)
            project_heads(1)

            def turn_tokens2(half):
                for m in range(HALF):
                    mm = pe.transpose(turn_ps[0:C2, 128 * m:128 * m + 128], normed[:, HALF * half + m, :], ident[:, :])
                mm.then_inc(turned2, 1)

            def fc1(r, half):
                for chunk in range(CHUNKS):
                    wait(pe, hidden_ok, CHUNKS * (r - 1) + chunk + 1)
                    product(fc1_ps[chunk][:, :], lambda part: wfc1_r[:, part, 128 * chunk:128 * chunk + 128],
                            lambda part: tokens2_t[:, half, part, :]).then_inc(fc1_mm, 1)

            def fc2(half):
                for m in range(HALF):
                    out_m = fc2_ps[half][:, C2 * m:C2 * m + C2]
                    for chunk in range(CHUNKS):
                        mm = pe.matmul(out_m, hidden[:, half, chunk, 128 * m:128 * m + 128],
                                       wfc2[:, chunk, :], start=(chunk == 0), stop=(chunk == CHUNKS - 1))
                mm.then_inc(fc2_mm, 1)

            def back(n, first, last):
                for half in range(2):
                    r = 2 * n + half
                    wait(pe, tokens2_t_ok, r + 1)
                    fc1(r, half)
                    if not (last and half == 1):
                        wait(pe, normed2_ok, r + 2)
                        turn_tokens2(1 - half)
                    if not (first and half == 0):
                        wait(pe, hidden_ok, CHUNKS * r)
                        fc2(1 - half)

            pe.wait_ge(x2_ok, 2 * BATCHES)
            pe.wait_ge(normed2_ok, 1)
            turn_tokens2(0)
            batches(pe, back)
            pe.wait_ge(hidden_ok, CHUNKS * 2 * BATCHES)
            pe.wait_ge(out_ok, 2 * BATCHES - 2)
            fc2(1)

        @block.scalar
        def _(act):
            def tokens_out(bank, half):
                act.activation(token_view(half), bank[0:C2, :].rearrange("c (j t) -> c j t", j=HALF),
                               ACT.Copy).then_inc(tokens_t_ok, 1)

            def probs_t_out():
                act.activation(probs_t[:, :, :], probs_t_ps[:, 0:HEADS * 128].rearrange("p (h q) -> p h q", h=HEADS),
                               ACT.Copy).then_inc(probs_t_ok, 1)

            def k_out():
                for h in range(HEADS):
                    rows = slice(2 * HD * h, 2 * HD * h + 2 * HD)
                    ins = act.activation(k_blocks[rows, :, h, :],
                                         kv_ps[rows, 0:2 * TOK].rearrange("p (a t) -> p a t", a=2), ACT.Copy)
                ins.then_inc(k_ok, 1)

            def v_out(k):
                for a in range(2):
                    rows = slice(TOK * a, TOK * a + TOK)
                    dst = v_blocks[rows, k % V_BUFS, :, 0:MIX - 2].rearrange("p h (b a d) -> p b h a d", b=2, a=2)
                    ins = act.activation(dst[:, :, :, a, :],
                                         kv_ps[rows, 128:128 + C2].rearrange("p (b h d) -> p b h d", b=2, h=HEADS), ACT.Copy)
                ins.then_inc(v_ok, 1)

            def exp(k):
                act.activation(probs[:, :, :, :].rearrange("p h a t -> p a h t"),
                               scores_ps[k % 2][:, 0:2 * HEADS * TOK].rearrange("p (a h t) -> p a h t", a=2, h=HEADS),
                               ACT.Exp).then_inc(probs_ok, 1)

            def heads_out(k):
                act.activation(heads_t[0:C2, :, 2 * WIN * k:2 * WIN * k + 2 * WIN],
                               heads_t_ps[0:C2, 0:128].rearrange("c (bi j) -> c j bi", j=WIN), ACT.Copy
                               ).then_inc(heads_t_ok, 1)

            def heads_of(g, k):
                wait(act, heads_turned, g + 1)
                heads_out(k % QUADS)

            def body(n, first, last):
                g0 = QUADS * n
                for k in range(QUADS):
                    if not (first and k == 0):
                        wait(act, probs_turned, g0 + k)
                        probs_t_out()
                    if k == 7 and not last:
                        heads_of(g0 + k - 3, k - 3)
                    if not (last and k == QUADS - 1):
                        wait(act, kv_mm, g0 + k + 2)
                        k_out()
                    wait(act, less_max_mm, g0 + k + 1)
                    exp(k)
                    if not (last and k == QUADS - 1):
                        v_out(k + 1)
                    if not (first and k < 2) and not (k == 6 and not last):
                        heads_of(g0 + k - 2, k - 2)
                    if k == 6 and not last:
                        wait(act, turned, 2 * n + 4)
                        wait(act, q_mm, g0 + QUADS)
                        tokens_out(turn_ps, 0)
                        tokens_out(heads_t_ps, 1)

            act.wait_ge(blocks_zeroed, 1)
            act.wait_ge(turned, 1)
            tokens_out(turn_ps, 0)
            act.wait_ge(turned, 2)
            tokens_out(heads_t_ps, 1)
            act.wait_ge(kv_mm, 1)
            k_out()
            v_out(0)
            batches(act, body)
            total = QUADS * BATCHES
            act.wait_ge(probs_turned, total)
            probs_t_out()
            heads_of(total - 2, QUADS - 2)
            heads_of(total - 1, QUADS - 1)

            def tokens2_out(half):
                act.activation(tokens2_t[0:C2, half, HIGH, :], turn_ps[0:C2, :], ACT.Copy).then_inc(tokens2_high, 1)

            def back(n, first, last):
                for half in range(2):
                    r = 2 * n + half
                    for chunk in range(CHUNKS):
                        wait(act, fc1_mm, CHUNKS * r + chunk + 1)
                        act.activation(hidden[:, half, chunk, :], fc1_ps[chunk][:, :], ACT.Gelu
                                       ).then_inc(hidden_ok, 1)
                    if not (last and half == 1):
                        wait(act, turned2, r + 2)
                        tokens2_out(1 - half)

            act.wait_ge(turned2, 1)
            tokens2_out(0)
            batches(act, back)

        @block.vector
        def _(dve):
            def take_stats(source, groups):
                for group in groups:
                    ins = dve.bn_stats(stats[:, group, :], source[:, group, :])
                return ins

            x_groups = x_in[:, :].rearrange("p (g c) -> p g c", c=C)

            def stats_back(n, part):
                return take_stats(x2_batch(n).rearrange("p a j c -> p (a j) c"), range(8 * part, 8 * part + 8))

            dve.wait_ge(x_loaded, 16 * QUADS)
            take_stats(x_groups, range(GROUPS)).then_inc(stats_ok, 1)
            dve.memset(tokens_t[C2:C2 + 1, :, :], 1.0)
            for part, value in ((HIGH, 1.0), (LOW, 0.0)):
                dve.memset(tokens2_t[C2:C2 + 1, :, part, :].bitcast(F32), value)
            dve.memset(heads_t[C2:C2 + 1, :, :], 1.0)
            dve.memset(k_blocks[:, :, :, :], 0.0)
            dve.memset(v_blocks[:, :, :, :], 0.0).then_inc(setup_dve, 1)
            dve.wait_ge(setup_dve, 1)
            for a in range(2):
                ins = dve.memset(v_blocks[TOK * a:TOK * a + TOK, :, :, MIX - 2 + a:MIX - 1 + a], 1.0)
            ins.then_inc(blocks_zeroed, 1)
            dve.wait_ge(consts_made, 1)
            dve.tensor_reduce(q_mask[:, :], row_mask[:, :, :].rearrange("p h b -> p b h"), AX.X, ALU.add)
            dve.tensor_copy(ident_r[:, :], ident[:, :])
            dve.tensor_copy(flip_r[:, :], flip[:, :, :].rearrange("p b q -> p (b q)"))
            dve.wait_ge(weights_in, 16 * (N_WEIGHT_DMAS))
            pos_flat = pos_in[:, :, :, :].rearrange("p h i j -> p (h i j)")
            dve.tensor_scalar(wqkv[0:C2, :], wqkv_in[:, :], gains[:, 0:1], None, ALU.mult)
            dve.tensor_scalar(wfc1[0:C2, :], wfc1_in[:, :], gains[:, 1:2], None, ALU.mult)
            dve.tensor_copy(pos_high[:, :], pos_flat).then_inc(setup_dve, 1)
            dve.wait_ge(bias_mm, 1)
            dve.tensor_tensor(wqkv[C2:C2 + 1, :], q_ps[C2:C2 + 1, 0:3 * C2], bias_row[C2:C2 + 1, 0:3 * C2], ALU.add)
            dve.tensor_tensor(wfc1[C2:C2 + 1, :], kv_ps[C2:C2 + 1, 0:2 * HID],
                              bias_row[C2:C2 + 1, 3 * C2:3 * C2 + 2 * HID], ALU.add).then_inc(setup_dve, 1)
            dve.wait_ge(setup_dve, 3)
            for a in range(2):
                dve.tensor_copy(pos[0:TOK, a, :], pos_high[0:TOK, :].bitcast(F32))
                ins = dve.tensor_tensor(pos[TOK:2 * TOK, a, :], pos_flat[TOK:2 * TOK, :],
                                        pos_high[TOK:2 * TOK, :].bitcast(F32), ALU.subtract)
            ins.then_inc(weights_ok, 1)
            dve.tensor_copy(wfc1_r[:, HIGH, :], wfc1[:, :]).then_inc(setup_dve, 1)
            dve.wait_ge(setup_dve, 4)
            dve.tensor_tensor(wfc1_r[:, LOW, :], wfc1[:, :], wfc1_r[:, HIGH, :].bitcast(F32), ALU.subtract
                              ).then_inc(weights_ok, 1)

            def q_out():
                dve.tensor_tensor(
                    q_blocks[:, :, :, :],
                    broadcast(q_ps[0:C2, 0:2 * TOK].rearrange("p (a q) -> p a q", a=2), 2, 2),
                    broadcast(broadcast(q_mask[:, :], 1, 2), 3, TOK), ALU.mult).then_inc(q_ok, 1)

            def row_max(k):
                dve.tensor_reduce(neg_max[:, :], scores_ps[k % 2][:, 0:2 * HEADS * TOK].rearrange("p (r t) -> p r t", t=TOK),
                                  AX.X, ALU.max, negate=True).then_inc(max_ok, 1)

            def normalise(g, k):
                mixed = mixed_ps[:, 0:HEADS * MIX].rearrange("p (h m) -> p h m", h=HEADS)
                dve.reciprocal(inv_sum[:, :, :], mixed[:, :, MIX - 2:MIX]).then_inc(inv_ok, 1)
                dve.wait_ge(inv_ok, g + 1)
                for b in range(2):
                    rows = slice(TOK * b, TOK * b + TOK)
                    own = mixed[rows, :, 2 * HD * b:2 * HD * b + 2 * HD].rearrange("p h (a d) -> p h a d", a=2)
                    ins = dve.tensor_tensor(heads[rows, k % 2, :, :, :].rearrange("p a h d -> p h a d"), own,
                                            broadcast(inv_sum[rows, :, :], 3, HD), ALU.mult)
                ins.then_inc(heads_ok, 1)

            def add_proj(n, half):
                tokens = x2_half(n, half)
                dve.tensor_tensor(tokens, turn_ps[:, 0:HALF * C2].rearrange("p (j a c) -> p j a c", j=HALF, a=2),
                                  tokens, ALU.add).then_inc(x2_ok, 1)

            def body(n, first, last):
                g0 = QUADS * n
                for k in range(QUADS):
                    wait(dve, scores_mm, g0 + k + 1)
                    row_max(k)
                    if k == 2 and not first:
                        dve.wait_ge(res_loaded, 64 * n)
                        dve.wait_ge(proj_mm, 2 * n - 1)
                        add_proj(n - 1, 0)
                    if not (last and k == QUADS - 1):
                        wait(dve, q_mm, g0 + k + 2)
                        q_out()
                    if k == 2 and not first:
                        dve.wait_ge(proj_mm, 2 * n)
                        add_proj(n - 1, 1)
                    if not (first and k == 0):
                        wait(dve, mixed_mm, g0 + k)
                        normalise(g0 + k - 1, k - 1)
                    if last and k in (0, 4):
                        if k == 0:
                            dve.wait_ge(small_step, SMALL_STEPS * (BATCHES - 1) + 3)
                        else:
                            dve.wait_ge(small2_step, 3)
                        dve.wait_ge(x2_ok, 2 * (k // 4) + 2)
                        stats_back(k // 4, 0)
                        stats_back(k // 4, 1).then_inc(stats2_ok, 1)
                    if not last:
                        if k == 0:
                            wait(dve, small_step, SMALL_STEPS * n + 3)
                            dve.wait_ge(x_loaded, 16 * QUADS * (n + 2))
                        if k < 3:
                            ins = take_stats(x_groups, range(6 * k, min(6 * k + 6, GROUPS)))
                            if k == 2:
                                ins.then_inc(stats_ok, 1)

            dve.wait_ge(q_mm, 1)
            q_out()
            batches(dve, body)
            total = QUADS * BATCHES
            dve.wait_ge(mixed_mm, total)
            normalise(total - 1, QUADS - 1)
            dve.wait_ge(res_loaded, 64 * BATCHES)
            for half in range(2):
                dve.wait_ge(proj_mm, 2 * BATCHES - 1 + half)
                add_proj(BATCHES - 1, half)

            def tokens2_rest(half):
                dve.tensor_tensor(tokens2_t[0:C2, half, LOW, :], turn_ps[0:C2, :],
                                  tokens2_t[0:C2, half, HIGH, :].bitcast(F32), ALU.subtract).then_inc(tokens2_t_ok, 1)

            def add_mlp(n, half):
                tokens = x2_half(n, half)
                dve.tensor_tensor(tokens, fc2_ps[half][:, 0:HALF * C2].rearrange("p (j a c) -> p j a c", j=HALF, a=2),
                                  tokens, ALU.add).then_inc(out_ok, 1)

            def back(n, first, last, more):
                for half in range(2):
                    r = 2 * n + half
                    if half == 1 and more:
                        wait(dve, small2_step, SMALL_STEPS * (n + 1) + 3)
                        stats_back(n + 2, 0)
                        stats_back(n + 2, 1).then_inc(stats2_ok, 1)
                    if not (last and half == 1):
                        wait(dve, tokens2_high, r + 2)
                        tokens2_rest(1 - half)
                    if half == 0:
                        wait(dve, normed2_ok, 2 * n + 2)
                        residual = x2_batch(n).rearrange("p a j c -> p (a j) c")
                        dve.tensor_tensor(residual, residual, broadcast(fc2_bias[:, :], 1, GROUPS),
                                          ALU.add).then_inc(biased2_ok, 1)
                    if not (first and half == 0):
                        if half == 1:
                            wait(dve, biased2_ok, n + 1)
                        wait(dve, fc2_mm, r)
                        add_mlp(n if half else n - 1, 1 - half)

            dve.wait_ge(tokens2_high, 1)
            tokens2_rest(0)
            back(0, True, False, True)
            with dve.Fori(1, BATCHES - 2) as n:
                back(n, False, False, True)
            back(BATCHES - 2, False, False, False)
            back(BATCHES - 1, False, True, False)
            dve.wait_ge(fc2_mm, 2 * BATCHES)
            add_mlp(BATCHES - 1, 1)


_P = "L0_conv_"
_INS = ["x"] + [_P + n for n in ("norm1_g", "norm1_b", "qkv_w", "qkv_b", "proj_w", "proj_b", "rel_bias_table",
                                 "norm2_g", "norm2_b", "fc1_w", "fc1_b", "fc2_w", "fc2_b")]


def kernel(**inputs):
    import concourse.bacc as bacc
    from concourse.bass_utils import run_bass_kernel_spmd

    nc = bacc.Bacc("TRN2", target_bir_lowering=False, num_devices=1)
    arrays, args = {}, []
    for name in _INS:
        a = np.asarray(inputs[name])
        if name.endswith("rel_bias_table"):
            a = a[::-1].T
        a = np.ascontiguousarray(a)
        arrays[f"in_{name}"] = a
        args.append(nc.dram_tensor(f"in_{name}", a.shape, mybir.dt.from_np(a.dtype), kind="ExternalInput").ap())
    args.append(nc.dram_tensor("out", (IMAGES, H, W, C), F32, kind="ExternalOutput").ap())
    swin_block(nc, *args)
    r = run_bass_kernel_spmd(nc, [arrays], core_ids=[0])
    return r.results[0]["out"]
```

```python
from contextlib import ExitStack

import numpy as np

import concourse.bass as bass
from concourse import mybir
from concourse.alu_op_type import AluOpType as ALU

F32 = mybir.dt.float32
F32R = mybir.dt.float32r
ACT = mybir.ActivationFunctionType
AX = mybir.AxisListType

IMAGES, H, W, C = 4, 128, 128, 48
WIN = 8
TOK = WIN * WIN
HEADS = 3
HD = C // HEADS
HID = 4 * C
SCALE = HD ** -0.5
EPS = 1e-5
STRIPES = IMAGES * H // WIN
BATCHES = STRIPES // 2
QUADS = 8
HALF = 4
C2 = 2 * C
ROW = 2 * WIN * C
REL = 2 * WIN - 1
TABLE = REL * REL
CHUNKS = 2 * HID // 128
MIX = 2 * 2 * HD + 2
V_BUFS = 4
HIGH, LOW = 0, 1
PARTS = ((HIGH, LOW), (LOW, HIGH), (HIGH, HIGH))
GROUPS = 2 * WIN
PAD = 64


def swin_block(nc, x, n1g, n1b, qkvw, qkvb, projw, projb, table, n2g, n2b, w1, b1, w2, b2, out):
    with ExitStack() as ctx:
        def sb(name, shape, dtype=F32):
            return ctx.enter_context(nc.sbuf_tensor(name, shape, dtype))

        def ps(name):
            return ctx.enter_context(nc.psum_tensor(name, [128, 512], F32))

        def sem(name):
            return ctx.enter_context(nc.semaphore(name))

        x_front = x.rearrange("m (s i) (a q bj) c -> (m s) q a i (bj c)", i=WIN, a=2, bj=2 * WIN)
        x_back = x.rearrange("m (s i) (a qb j) c -> (m s) a qb i (j c)", i=WIN, a=2, j=WIN)
        out_back = out.rearrange("m (s i) (a qb j) c -> (m s) a qb i (j c)", i=WIN, a=2, j=WIN)

        x2 = sb("x2", [128, BATCHES * ROW])
        x_in = sb("x_in", [128, ROW])
        stats = sb("stats", [128, GROUPS, 6])
        small = sb("small", [128, 8, GROUPS])
        rstd = sb("rstd", [128, GROUPS])
        minus_half = sb("minus_half", [128, GROUPS])
        fourth = sb("fourth", [128, GROUPS])
        centred = sb("centred", [128, GROUPS, C])
        normed = sb("normed", [128, WIN, C2])
        tokens_t = sb("tokens_t", [C2 + 1, QUADS, 2 * TOK])
        tokens_r = sb("tokens_r", [C2 + 1, 2, QUADS, 2 * TOK], F32R)
        q_blocks = sb("q_blocks", [C2, 2, 2, 2, TOK])
        k_blocks = sb("k_blocks", [C2, 2, 2, HEADS, TOK])
        v_blocks = sb("v_blocks", [128, V_BUFS, HEADS, MIX])
        row_top = sb("row_top", [128, 2, 2 * HEADS])
        lowered = sb("lowered", [128, 2, HEADS, TOK])
        probs = sb("probs", [128, 2, HEADS, 2, TOK])
        probs_t = sb("probs_t", [128, HEADS, 128])
        inv_sum = sb("inv_sum", [128, HEADS, 2])
        heads = sb("heads", [128, 2, 2, HEADS, HD])
        heads_t = sb("heads_t", [C2 + 1, WIN, QUADS * 2 * WIN])
        normed2 = sb("normed2", [128, WIN, 2, PAD])
        tokens2_high = sb("tokens2_high", [128, 2, HALF * 128], F32R)
        tokens2_both = sb("tokens2_both", [128, 2, 2, HALF * 128], F32R)
        hidden = sb("hidden", [128, 2, CHUNKS, HALF * 128])

        wqkv = sb("wqkv", [C2 + 1, 3 * C2])
        wqk_r = sb("wqk_r", [C2 + 1, 2, 2 * C2], F32R)
        wqkv_in = sb("wqkv_in", [C2, 3 * C])
        wproj = sb("wproj", [C2 + 1, C2])
        wfc1 = sb("wfc1", [128, HID])
        wfc1_in = sb("wfc1_in", [128, HID])
        fc1_gain = sb("fc1_gain", [128, 1])
        fc1_shift = sb("fc1_shift", [C, 128])
        wproj_in = sb("wproj_in", [C2, C])
        wfc1_high = sb("wfc1_high", [128, HID], F32R)
        wfc1_shared = sb("wfc1_shared", [128, 2, 128], F32R)
        wfc1_low = sb("wfc1_low", [128, 2 * HID], F32R)
        wfc2 = sb("wfc2", [128, CHUNKS, C2])
        fc2_bias = sb("fc2_bias", [128, C])
        gains = sb("gains", [C2, 1])
        shifts = sb("shifts", [C2, C2 + 1])
        bias_row = sb("bias_row", [C2 + 1, 3 * C])
        window_mask = sb("window_mask", [C2, 2])
        window_gains = sb("window_gains", [C2, 2])
        pos_in = sb("pos_in", [TOK, HEADS, REL * (WIN - 1) + WIN])
        pos_all = sb("pos_all", [128, HEADS, WIN, WIN])
        pos_high = sb("pos_high", [128, HEADS * TOK], F32R)
        pos = sb("pos", [128, 2, HEADS * TOK], F32R)
        ident = sb("ident", [128, 128])
        flip = sb("flip", [128, 2, TOK])
        flip_r = sb("flip_r", [128, 2 * TOK], F32R)
        row_mask = sb("row_mask", [C2, HEADS, 2])
        q_mask = sb("q_mask", [C2, 2])

        turn_ps = ps("turn_ps")
        q_ps = ps("q_ps")
        kv_ps = ps("kv_ps")
        scores_ps = [ps("scores_ps0"), ps("scores_ps1")]
        probs_t_ps = ps("probs_t_ps")
        mixed_ps = ps("mixed_ps")
        heads_t_ps = ps("heads_t_ps")
        fc1_ps = [q_ps, kv_ps, probs_t_ps]
        fc2_ps = scores_ps

        zeroed = sem("zeroed")
        qkv_in = sem("qkv_in")
        table_in = sem("table_in")
        weights_in = sem("weights_in")
        qkv_ok = sem("qkv_ok")
        pos_ok = sem("pos_ok")
        weights_ok = sem("weights_ok")
        consts_made = sem("consts_made")
        pool_step = sem("pool_step")
        setup_dve = sem("setup_dve")
        blocks_zeroed = sem("blocks_zeroed")
        bias_mm = sem("bias_mm")
        x_loaded = sem("x_loaded")
        res_loaded = sem("res_loaded")
        stats_ok = sem("stats_ok")
        normed_ok = sem("normed_ok")
        small_step = sem("small_step")
        turned = sem("turned")
        tokens_high = sem("tokens_high")
        tokens_whole = sem("tokens_whole")
        tokens_low0 = sem("tokens_low0")
        tokens_low1 = sem("tokens_low1")
        q_mm = sem("q_mm")
        kv_mm = sem("kv_mm")
        q_ok = sem("q_ok")
        k_ok = sem("k_ok")
        v_ok = sem("v_ok")
        scores_mm = sem("scores_mm")
        max_ok = sem("max_ok")
        lowered_ok = sem("lowered_ok")
        probs_ok = sem("probs_ok")
        probs_turned = sem("probs_turned")
        first_t_ok = sem("first_t_ok")
        probs_t_ok = sem("probs_t_ok")
        mixed_mm = sem("mixed_mm")
        inv_ok = sem("inv_ok")
        heads_ok = sem("heads_ok")
        heads_turned = sem("heads_turned")
        heads_t_ok = sem("heads_t_ok")
        proj_mm = sem("proj_mm")
        x2_ok = sem("x2_ok")
        stats2_ok = sem("stats2_ok")
        normed2_ok = sem("normed2_ok")
        biased2_ok = sem("biased2_ok")
        small2_step = sem("small2_step")
        turned2 = sem("turned2")
        tokens2_high_ok = sem("tokens2_high_ok")
        tokens2_block_ok = sem("tokens2_block_ok")
        tokens2_t_ok = sem("tokens2_t_ok")
        fc1_mm = sem("fc1_mm")
        hidden_ok = sem("hidden_ok")
        fc2_mm = sem("fc2_mm")
        out_ok = sem("out_ok")
        stored = sem("stored")

        QKV_DMAS, TABLE_DMAS, WEIGHT_DMAS = 6, WIN, 17
        SMALL_STEPS = 10
        STATS_CUT = 5

        def wait(eng, semaphore, count):
            if not (isinstance(count, int) and count <= 0):
                eng.wait_ge(semaphore, count)

        def batches(eng, body):
            body(0, True, False)
            with eng.Fori(1, BATCHES - 1) as n:
                body(n, False, False)
            body(BATCHES - 1, False, True)

        def x2_batch(n):
            return x2[:, bass.ds(n * ROW, ROW)].rearrange("p (a j c) -> p a j c", a=2, j=WIN)

        def x2_half(n, half):
            return x2_batch(n)[:, :, HALF * half:HALF * half + HALF, :].rearrange("p a j c -> p j a c")

        def broadcast(ap, axis, count):
            shape = list(ap.shape)
            shape.insert(axis, count)
            return ap.unsqueeze(axis).to_broadcast(shape)

        def token_view(tokens, half):
            view = tokens.rearrange("c k (ai j) -> c j (k ai)", j=WIN)
            return view[:, HALF * half:HALF * half + HALF, :]

        def tokens_low(eng, n, half):
            wait(eng, tokens_high, 2 * n + 1 + half)
            return eng.tensor_tensor(
                token_view(tokens_r[0:C2, LOW, :, :], half), token_view(tokens_t[0:C2, :, :], half),
                token_view(tokens_r[0:C2, HIGH, :, :], half).bitcast(F32), ALU.subtract)

        block = ctx.enter_context(nc.Block())

        @block.sync
        def _(sp):
            def load_front(n):
                for k in range(QUADS):
                    sp.dma_start(x_in[2 * WIN * k:2 * WIN * k + 2 * WIN, :],
                                 x_front[2 * n + k // HALF, k % HALF]).then_inc(x_loaded, 16)

            load_front(0)
            sp.wait_ge(zeroed, 1)
            counts = {qkv_in: 0, table_in: 0, weights_in: 0}

            def load(dst, src, done):
                sp.dma_start(dst, src).then_inc(done, 16)
                counts[done] += 1

            def row(v):
                return v.rearrange("(o n) -> o n", o=1)

            def column(v):
                return v.rearrange("(n o) -> n o", o=1)

            def load_twice(dst, src, done):
                for b in range(2):
                    load(dst[C * b:C * b + C, :], src, done)

            load_twice(wqkv_in[:, :], qkvw, qkv_in)
            load_twice(gains[:, 0:1], column(n1g), qkv_in)
            load(shifts[0:C, C2:C2 + 1], column(n1b), qkv_in)
            load(bias_row[C2:C2 + 1, 0:3 * C], row(qkvb), qkv_in)
            for pi in range(WIN):
                load(pos_in[WIN * pi:WIN * pi + WIN, :, :], bass.AP(
                    table.tensor, REL * pi, [[1, WIN], [TABLE, HEADS], [1, REL * (WIN - 1) + WIN]]), table_in)
            for a in range(2):
                at = PAD * a
                load(wfc1_in[at:at + C, :], w1, weights_in)
                load(wfc1_in[at + C:at + C + 1, :], row(b1), weights_in)
                load(fc1_gain[at:at + C, :], column(n2g), weights_in)
                load(fc1_shift[:, at + C:at + C + 1], column(n2b), weights_in)
            load_twice(wproj_in[:, :], projw, weights_in)
            for b in range(2):
                load(wproj[C2:C2 + 1, C * b:C * b + C], row(projb), weights_in)
                at = HID * b
                while at < HID * (b + 1):
                    end = min(HID * (b + 1), (at // 128 + 1) * 128)
                    load(wfc2[at % 128:at % 128 + end - at, at // 128, C * b:C * b + C],
                         w2[at - HID * b:end - HID * b, :], weights_in)
                    at = end
            load(fc2_bias[:, :], row(b2).to_broadcast([128, C]), weights_in)
            assert tuple(counts.values()) == (QKV_DMAS, TABLE_DMAS, WEIGHT_DMAS), counts

            def body(n, first, last):
                if not last:
                    wait(sp, small_step, SMALL_STEPS * n + SMALL_STEPS - 1)
                    load_front(n + 1)
                wait(sp, x2_ok, 2 * n)
                for s in range(2):
                    for a in range(2):
                        sp.dma_start(x2[64 * s:64 * s + 64, bass.ds(n * ROW + a * (ROW // 2), ROW // 2)],
                                     x_back[2 * n + s, a]).then_inc(res_loaded, 16)

            batches(sp, body)

            with sp.Fori(0, BATCHES) as n:
                sp.wait_ge(out_ok, 2 * n + 2)
                for s in range(2):
                    for a in range(2):
                        sp.dma_start(out_back[2 * n + s, a],
                                     x2[64 * s:64 * s + 64, bass.ds(n * ROW + a * (ROW // 2), ROW // 2)]
                                     ).then_inc(stored, 16)
            sp.wait_ge(stored, 64 * BATCHES)

        def layer_norm(pool, n, source, step, stats_sem):
            done = SMALL_STEPS * n
            mean_even, mean_odd, sq_even, sq_odd = (stats[:, :, f] for f in (1, 4, 2, 5))
            total, gap, squares, gap2, mean, scaled, quarter, variance = (small[:, f, :] for f in range(8))
            pool.wait_ge(stats_sem, n + 1)
            pool.tensor_tensor(total, mean_even, mean_odd, ALU.add).then_inc(step, 1)
            pool.tensor_tensor(gap, mean_even, mean_odd, ALU.subtract).then_inc(step, 1)
            pool.tensor_tensor(squares, sq_even, sq_odd, ALU.add).then_inc(step, 1)
            pool.wait_ge(step, done + 3)
            pool.tensor_tensor(gap2, gap, gap, ALU.mult).then_inc(step, 1)
            pool.tensor_scalar(mean, total, 0.5, None, ALU.mult).then_inc(step, 1)
            pool.tensor_scalar(scaled, squares, 1.0 / C, EPS, ALU.mult, ALU.add).then_inc(step, 1)
            pool.wait_ge(step, done + 6)
            pool.tensor_tensor(quarter, gap2, fourth[:, :], ALU.mult).then_inc(step, 1)
            pool.wait_ge(step, done + 7)
            pool.tensor_tensor(variance, scaled, quarter, ALU.add).then_inc(step, 1)
            pool.tensor_tensor(centred[:, :, :], source, broadcast(mean, 2, C), ALU.subtract).then_inc(step, 1)
            pool.wait_ge(step, done + 8)
            pool.tensor_tensor(rstd[:, :], variance, minus_half[:, :], ALU.pow).then_inc(step, 1)
            pool.wait_ge(step, done + 10)

        def scale_half(pool, half, target):
            js = slice(HALF * half, HALF * half + HALF)
            return pool.tensor_tensor(
                target[:, :, js, :],
                centred[:, :, :].rearrange("p (w j) c -> p w j c", w=2)[:, :, js, :],
                broadcast(rstd[:, :].rearrange("p (w j) -> p w j", w=2)[:, :, js], 3, C), ALU.mult)

        @block.gpsimd
        def _(pool):
            pool.memset(wfc2[:, :, :], 0.0)
            pool.memset(wfc1_in[:, :], 0.0)
            pool.memset(fc1_gain[:, :], 1.0)
            pool.memset(fc1_shift[:, :], 0.0)
            pool.memset(shifts[:, :], 0.0).then_inc(zeroed, 1)
            pool.memset(ident[:, :], 0.0)
            pool.memset(flip[:, :, :], 0.0)
            pool.memset(minus_half[:, :], -0.5)
            pool.memset(fourth[:, :], 0.25)
            pool.memset(window_mask[:, :], 1.0)
            pool.memset(row_mask[:, :, :], SCALE).then_inc(pool_step, 1)
            pool.wait_ge(pool_step, 1)
            pool.affine_select(out=ident[:, :], in_=ident[:, :], compare_op=ALU.not_equal, fill=1.0,
                               base=0, pattern=[[-1, 128]], channel_multiplier=1)
            pool.affine_select(out=flip[:, :, :], in_=flip[:, :, :], compare_op=ALU.not_equal, fill=1.0,
                               base=1 - TOK, pattern=[[0, 2], [1, TOK]], channel_multiplier=1)
            pool.affine_select(out=window_mask[:, :], in_=window_mask[:, :], compare_op=ALU.is_ge, fill=0.0,
                               base=0, pattern=[[-C, 2]], channel_multiplier=1)
            pool.affine_select(out=row_mask[:, :, :], in_=row_mask[:, :, :], compare_op=ALU.is_ge, fill=0.0,
                               base=0, pattern=[[-2 * HD, HEADS], [-HD, 2]], channel_multiplier=1).then_inc(pool_step, 1)
            pool.wait_ge(pool_step, 2)
            pool.affine_select(out=flip[:, :, :], in_=flip[:, :, :], compare_op=ALU.not_equal, fill=1.0,
                               base=1 - 2 * TOK, pattern=[[0, 2], [1, TOK]], channel_multiplier=1)
            pool.affine_select(out=window_mask[:, :], in_=window_mask[:, :], compare_op=ALU.is_ge, fill=0.0,
                               base=C - 1, pattern=[[C, 2]], channel_multiplier=-1)
            pool.affine_select(out=row_mask[:, :, :], in_=row_mask[:, :, :], compare_op=ALU.is_ge, fill=0.0,
                               base=HD - 1, pattern=[[2 * HD, HEADS], [HD, 2]], channel_multiplier=-1
                               ).then_inc(consts_made, 1)

            def norm_front(n):
                layer_norm(pool, n, x_in[:, :].rearrange("p (g c) -> p g c", c=C), small_step, stats_ok)
                for half in range(2):
                    wait(pool, turned, 2 * n - 1 + half)
                    scale_half(pool, half, normed[:, :, :].rearrange("p j (w c) -> p w j c", w=2)).then_inc(normed_ok, 1)

            norm_front(0)
            with pool.Fori(1, BATCHES) as n:
                norm_front(n)
                tokens_low(pool, n, 0).then_inc(tokens_low0, 1)

            def norm_back(n):
                layer_norm(pool, n, x2_batch(n).rearrange("p a j c -> p (a j) c"), small2_step, stats2_ok)
                for half in range(2):
                    wait(pool, turned2, 2 * n - 1 + half)
                    target = normed2[:, :, :, 0:C].rearrange("p j w c -> p w j c")
                    scale_half(pool, half, target).then_inc(normed2_ok, 1)

            norm_back(0)
            with pool.Fori(1, BATCHES) as n:
                norm_back(n)

        @block.tensor
        def _(pe):
            def turn_tokens(half):
                bank = (turn_ps, q_ps)[half]
                for m in range(HALF):
                    mm = pe.transpose(bank[0:C2, 128 * m:128 * m + 128], normed[:, HALF * half + m, :], ident[:, :])
                mm.then_inc(turned, 1)

            def product(out, left, right):
                for i, (p, q) in enumerate(PARTS):
                    mm = pe.matmul(out, left(p), right(q), start=(i == 0), stop=(i == len(PARTS) - 1))
                return mm

            def project_v(k):
                for m in range(2):
                    pe.matmul(kv_ps[:, 256 + C2 * m:256 + C2 * m + C2], tokens_t[:, k + m, :], wqkv[:, 2 * C2:3 * C2],
                              start=True, stop=True)

            def project_qk(k):
                def tokens(part):
                    return tokens_r[:, part, k:k + 2, :].rearrange("p k t -> p (k t)")

                def weights(m):
                    return lambda part: wqk_r[:, part, C2 * m:C2 * m + C2]

                product(q_ps[0:C2, 0:4 * TOK], weights(0), tokens).then_inc(q_mm, 1)
                product(kv_ps[0:C2, 0:4 * TOK], weights(1), tokens).then_inc(kv_mm, 1)

            def scores(k):
                bank = scores_ps[k % 2]
                pe.matmul(bank[:, 0:2 * HEADS * TOK], flip_r[:, :], pos[:, :, :].rearrange("p a n -> p (a n)"),
                          start=True, stop=False, skip_group_check=True)
                for a in range(2):
                    at = HEADS * TOK * a
                    mm = pe.matmul(bank[:, at:at + HEADS * TOK], q_blocks[:, k % 2, a, :, :].rearrange("p b q -> p (b q)"),
                                   k_blocks[:, k % 2, a, :, :].rearrange("p h t -> p (h t)"),
                                   start=False, stop=True, skip_group_check=True)
                mm.then_inc(scores_mm, 1)

            def turn_probs(k):
                for h in range(HEADS):
                    mm = pe.transpose(probs_t_ps[:, 128 * h:128 * h + 128],
                                      probs[:, k % 2, h, :, :].rearrange("p a t -> p (a t)"), ident[:, :])
                mm.then_inc(probs_turned, 1)

            def mix(g, k):
                wait(pe, first_t_ok, g + 1)
                for h in range(HEADS):
                    if h == 1:
                        wait(pe, probs_t_ok, g + 1)
                    mm = pe.matmul(mixed_ps[:, MIX * h:MIX * h + MIX], probs_t[:, h, :], v_blocks[:, k % V_BUFS, h, :],
                                   start=True, stop=True)
                mm.then_inc(mixed_mm, 1)

            def turn_heads(k):
                pe.transpose(heads_t_ps[0:C2, 0:128], heads[:, k % 2, :, :, :].rearrange("p a h d -> p (a h d)"),
                             ident[:, :]).then_inc(heads_turned, 1)

            def project_heads(half):
                bank = (turn_ps, heads_t_ps)[half]
                for m in range(HALF):
                    mm = pe.matmul(bank[:, C2 * m:C2 * m + C2], heads_t[:, HALF * half + m, :], wproj[:, :],
                                   start=True, stop=True)
                mm.then_inc(proj_mm, 1)

            def turn_heads_of(g, k):
                wait(pe, heads_ok, g + 1)
                wait(pe, heads_t_ok, g)
                turn_heads(k)

            def turn_tokens2(half):
                for m in range(HALF):
                    mm = pe.transpose(turn_ps[:, 128 * m:128 * m + 128],
                                      normed2[:, HALF * half + m, :, :].rearrange("p w c -> p (w c)"), ident[:, :])
                mm.then_inc(turned2, 1)

            def fc1_chunk(r, half, chunk):
                wait(pe, hidden_ok, CHUNKS * (r - 1) + chunk + 1)
                bank = fc1_ps[chunk][:, :]
                pe.matmul(bank, wfc1_low[:, 128 * chunk:128 * chunk + 128], tokens2_high[:, half, :],
                          start=True, stop=False)
                terms = {0: ((wfc1_high[:, 0:128], 0),),
                         1: ((wfc1_shared[:, 0, :], 0), (wfc1_shared[:, 1, :], 1)),
                         2: ((wfc1_high[:, HID - 128:HID], 1),)}[chunk]
                for weights, a in terms:
                    mm = pe.matmul(bank, weights, tokens2_both[:, half, a, :], start=False, stop=(weights is terms[-1][0]))
                mm.then_inc(fc1_mm, 1)

            def fc2(half):
                for m in range(HALF):
                    out_m = fc2_ps[half][:, C2 * m:C2 * m + C2]
                    for chunk in range(CHUNKS):
                        mm = pe.matmul(out_m, hidden[:, half, chunk, 128 * m:128 * m + 128],
                                       wfc2[:, chunk, :], start=(chunk == 0), stop=(chunk == CHUNKS - 1))
                mm.then_inc(fc2_mm, 1)

            def body(n, first, last):
                g0 = QUADS * n

                def turn_older_probs(k):
                    if not (first and k < 2):
                        wait(pe, probs_ok, g0 + k - 1)
                        wait(pe, probs_t_ok, g0 + k - 2)
                        turn_probs(k)

                for k in range(QUADS):
                    if k % 2 == 0:
                        turn_older_probs(k)
                    wait(pe, q_ok, 4 * n + k // 2 + 1)
                    wait(pe, k_ok, g0 + k + 1)
                    wait(pe, lowered_ok, g0 + k - 1)
                    if k == 6 and not last:
                        wait(pe, normed_ok, 2 * n + 4)
                        turn_tokens(1)
                    scores(k)
                    if k == 3 and not first:
                        wait(pe, heads_t_ok, g0)
                        project_heads(0)
                        project_heads(1)
                    if k % 2 == 1:
                        ahead = not (last and k == QUADS - 1)
                        turn_older_probs(k)
                        wait(pe, v_ok, 4 * n + k // 2 + 1)
                        if ahead:
                            if k == QUADS - 1:
                                wait(pe, tokens_whole, 2 * n + 4)
                            project_v((k + 1) % QUADS)
                            if k == QUADS - 1:
                                wait(pe, tokens_low0, n + 2)
                                wait(pe, tokens_low1, n + 2)
                            project_qk((k + 1) % QUADS)
                    if not (first and k < 3):
                        if k == 3:
                            wait(pe, x2_ok, 2 * n)
                        turn_heads_of(g0 + k - 3, k - 3)
                    if first and k == 2:
                        wait(pe, weights_ok, 1)
                    if not (first and k < 2):
                        wait(pe, heads_ok, g0 + k - 2)
                        mix(g0 + k - 2, k - 2)
                    if k == 5 and not last:
                        wait(pe, normed_ok, 2 * n + 3)
                        turn_tokens(0)
                    if k == 5 and last:
                        wait(pe, normed2_ok, 1)
                        turn_tokens2(0)
                    if k == QUADS - 1 and last:
                        wait(pe, tokens2_t_ok, 1)
                        wait(pe, tokens2_block_ok, 1)
                        fc1_chunk(0, 0, 0)
                        fc1_chunk(0, 0, 1)
                        wait(pe, normed2_ok, 2)
                        turn_tokens2(1)

            pe.wait_ge(zeroed, 1)
            pe.wait_ge(qkv_in, 16 * QKV_DMAS)
            pe.matmul(probs_t_ps[0:C2 + 1, 0:3 * C], shifts[:, :], wqkv_in[:, :], start=True, stop=True
                      ).then_inc(bias_mm, 1)
            pe.wait_ge(consts_made, 1)
            pe.wait_ge(normed_ok, 1)
            turn_tokens(0)
            pe.wait_ge(normed_ok, 2)
            turn_tokens(1)
            pe.wait_ge(qkv_ok, 1)
            pe.wait_ge(tokens_whole, 2)
            project_v(0)
            pe.wait_ge(tokens_low0, 1)
            pe.wait_ge(tokens_low1, 1)
            project_qk(0)
            pe.wait_ge(weights_in, 16 * WEIGHT_DMAS)
            pe.matmul(mixed_ps[:, 0:HID], fc1_shift[:, :], wfc1_in[0:C, :], start=True, stop=True
                      ).then_inc(bias_mm, 1)
            pe.wait_ge(pos_ok, 1)
            batches(pe, body)
            total = QUADS * BATCHES
            for k in (QUADS - 2, QUADS - 1):
                g = total - QUADS + k
                pe.wait_ge(probs_ok, g + 1)
                pe.wait_ge(probs_t_ok, g)
                turn_probs(k)
                turn_heads_of(g - 1, k - 1)
                pe.wait_ge(heads_ok, g)
                mix(g, k)
            fc1_chunk(0, 0, CHUNKS - 1)
            turn_heads_of(total - 1, QUADS - 1)
            pe.wait_ge(heads_t_ok, total)
            pe.wait_ge(tokens2_t_ok, 2)
            pe.wait_ge(tokens2_block_ok, 2)
            project_heads(0)
            project_heads(1)

            def fc1(r, half):
                for chunk in range(CHUNKS):
                    fc1_chunk(r, half, chunk)

            def back(n, first, last):
                for half in range(2):
                    r = 2 * n + half
                    if first and half == 0:
                        continue
                    wait(pe, tokens2_t_ok, r + 1)
                    wait(pe, tokens2_block_ok, r + 1)
                    if first:
                        fc1(r, half)
                        wait(pe, x2_ok, 2 * BATCHES)
                    if not (last and half == 1):
                        wait(pe, normed2_ok, r + 2)
                        turn_tokens2(1 - half)
                    if not first:
                        fc1(r, half)
                    wait(pe, hidden_ok, CHUNKS * r)
                    fc2(1 - half)

            batches(pe, back)
            pe.wait_ge(hidden_ok, CHUNKS * 2 * BATCHES)
            pe.wait_ge(out_ok, 2 * BATCHES - 2)
            fc2(1)

        @block.scalar
        def _(act):
            def tokens_out(half):
                source = (turn_ps, q_ps)[half][0:C2, :].rearrange("c (j t) -> c j t", j=HALF)
                act.activation(token_view(tokens_t[0:C2, :, :], half), source, ACT.Copy).then_inc(tokens_whole, 1)
                act.activation(token_view(tokens_r[0:C2, HIGH, :, :], half), source, ACT.Copy).then_inc(tokens_high, 1)

            def probs_t_out():
                source = probs_t_ps[:, 0:HEADS * 128].rearrange("p (h q) -> p h q", h=HEADS)
                act.activation(probs_t[:, 0:1, :], source[:, 0:1, :], ACT.Copy).then_inc(first_t_ok, 1)
                act.activation(probs_t[:, 1:HEADS, :], source[:, 1:HEADS, :], ACT.Copy).then_inc(probs_t_ok, 1)

            def k_out(k):
                for h in range(HEADS):
                    rows = slice(2 * HD * h, 2 * HD * h + 2 * HD)
                    at = 2 * TOK * (k % 2)
                    ins = act.activation(k_blocks[rows, k % 2, :, h, :],
                                         kv_ps[rows, at:at + 2 * TOK].rearrange("p (a t) -> p a t", a=2), ACT.Copy)
                ins.then_inc(k_ok, 1)

            def v_out(k):
                for m in range(2):
                    for a in range(2):
                        rows = slice(TOK * a, TOK * a + TOK)
                        dst = v_blocks[rows, (k + m) % V_BUFS, :, 0:MIX - 2].rearrange("p h (b a d) -> p b h a d", b=2, a=2)
                        at = 256 + C2 * m
                        ins = act.activation(dst[:, :, :, a, :],
                                             kv_ps[rows, at:at + C2].rearrange("p (b h d) -> p b h d", b=2, h=HEADS), ACT.Copy)
                ins.then_inc(v_ok, 1)

            def exp(k):
                act.activation(probs[:, k % 2, :, :, :].rearrange("p h a t -> p a h t"), lowered[:, :, :, :],
                               ACT.Exp).then_inc(probs_ok, 1)

            def tokens2_out(half):
                act.activation(tokens2_high[:, half, :], turn_ps[:, :], ACT.Copy).then_inc(tokens2_block_ok, 1)
                for a in range(2):
                    rows = slice(PAD * a, PAD * a + PAD)
                    act.activation(tokens2_both[rows, half, a, :], turn_ps[rows, :], ACT.Copy).then_inc(tokens2_high_ok, 1)

            def heads_out(k):
                act.activation(heads_t[0:C2, :, 2 * WIN * k:2 * WIN * k + 2 * WIN],
                               heads_t_ps[0:C2, 0:128].rearrange("c (bi j) -> c j bi", j=WIN), ACT.Copy
                               ).then_inc(heads_t_ok, 1)

            def heads_of(g, k):
                wait(act, heads_turned, g + 1)
                heads_out(k % QUADS)

            def body(n, first, last):
                g0 = QUADS * n
                for k in range(QUADS):
                    ahead = k % 2 == 1 and not (last and k == QUADS - 1)
                    if not (first and k < 2):
                        wait(act, probs_turned, g0 + k - 1)
                        probs_t_out()
                    if k % 2 == 0 and not (first and k == 0):
                        k_out(k + 1)
                    if k == 6 and not last:
                        wait(act, turned, 2 * n + 4)
                        tokens_out(1)
                    if k % 2 == 0:
                        v_out(k)
                        if not (first and k < 3):
                            heads_of(g0 + k - 3, k - 3)
                    if ahead:
                        wait(act, kv_mm, 4 * n + k // 2 + 2)
                        k_out(k + 1)
                    wait(act, lowered_ok, g0 + k + 1)
                    exp(k)
                    if k % 2 == 1 and not (first and k < 3):
                        heads_of(g0 + k - 3, k - 3)
                    if k == 5 and last:
                        wait(act, turned2, 1)
                        tokens2_out(0)
                    if k == 5 and not last:
                        wait(act, turned, 2 * n + 3)
                        wait(act, kv_mm, 4 * n + 4)
                        tokens_out(0)

            act.wait_ge(consts_made, 1)
            act.activation(heads_t[C2:C2 + 1, :, :], broadcast(ident[C2:C2 + 1, :], 1, WIN), ACT.Copy, bias=1.0,
                           scale=0.0)
            for half in range(2):
                act.wait_ge(turned, half + 1)
                tokens_out(half)
            act.wait_ge(blocks_zeroed, 1)
            act.wait_ge(kv_mm, 1)
            k_out(0)
            k_out(1)
            batches(act, body)
            total = QUADS * BATCHES
            for k in (QUADS - 2, QUADS - 1):
                g = total - QUADS + k
                act.wait_ge(probs_turned, g + 1)
                probs_t_out()
                if k == QUADS - 2:
                    act.wait_ge(turned2, 2)
                    tokens2_out(1)
                heads_of(g - 1, k - 1)
            heads_of(total - 1, QUADS - 1)

            def back(n, first, last):
                for half in range(2):
                    r = 2 * n + half
                    if not (first and half == 0) and not (last and half == 1):
                        wait(act, turned2, r + 2)
                        tokens2_out(1 - half)
                    for chunk in range(CHUNKS):
                        wait(act, fc1_mm, CHUNKS * r + chunk + 1)
                        act.activation(hidden[:, half, chunk, :], fc1_ps[chunk][:, :], ACT.Gelu
                                       ).then_inc(hidden_ok, 1)

            batches(act, back)

        @block.vector
        def _(dve):
            def take_stats(source, groups):
                for group in groups:
                    ins = dve.bn_stats(stats[:, group, :], source[:, group, :])
                return ins

            x_groups = x_in[:, :].rearrange("p (g c) -> p g c", c=C)

            def stats_back(n, part):
                return take_stats(x2_batch(n).rearrange("p a j c -> p (a j) c"), range(8 * part, 8 * part + 8))

            dve.wait_ge(x_loaded, 16 * QUADS)
            take_stats(x_groups, range(GROUPS)).then_inc(stats_ok, 1)
            dve.memset(k_blocks[:, :, :, :, :], 0.0)
            dve.memset(v_blocks[:, :, :, :], 0.0).then_inc(setup_dve, 1)
            dve.memset(tokens_t[C2:C2 + 1, :, :], 1.0)
            for part, value in ((HIGH, 1.0), (LOW, 0.0)):
                dve.memset(tokens_r[C2:C2 + 1, part, :, :].bitcast(F32), value)
            dve.wait_ge(setup_dve, 1)
            for a in range(2):
                ins = dve.memset(v_blocks[TOK * a:TOK * a + TOK, :, :, MIX - 2 + a:MIX - 1 + a], 1.0)
            ins.then_inc(blocks_zeroed, 1)
            dve.wait_ge(consts_made, 1)
            dve.tensor_reduce(q_mask[:, :], row_mask[:, :, :].rearrange("p h b -> p b h"), AX.X, ALU.add)
            dve.tensor_copy(flip_r[:, :], flip[:, :, :].rearrange("p b q -> p (b q)"))

            dve.wait_ge(qkv_in, 16 * QKV_DMAS)
            dve.tensor_tensor(window_gains[:, :], gains[:, :].to_broadcast([C2, 2]), window_mask[:, :], ALU.mult
                              ).then_inc(setup_dve, 1)
            dve.wait_ge(setup_dve, 2)
            for b in range(2):
                for m in range(2):
                    at = C2 * m
                    dve.tensor_scalar(
                        wqkv[0:C2, at:at + C2].rearrange("p (h b d) -> p h b d", h=HEADS, b=2)[:, :, b, :],
                        wqkv_in[:, C * m:C * m + C].rearrange("p (h d) -> p h d", h=HEADS),
                        window_gains[:, b:b + 1], None, ALU.mult)
                at = 2 * C2 + C * b
                dve.tensor_scalar(wqkv[0:C2, at:at + C], wqkv_in[:, 2 * C:3 * C], window_gains[:, b:b + 1], None, ALU.mult)
            dve.wait_ge(bias_mm, 1)
            for m in range(2):
                source = slice(C * m, C * m + C)
                dve.tensor_tensor(wqkv[C2:C2 + 1, C2 * m:C2 * m + C2].rearrange("p (h b d) -> p h b d", h=HEADS, b=2),
                                  broadcast(probs_t_ps[C2:C2 + 1, source].rearrange("p (h d) -> p h d", h=HEADS), 2, 2),
                                  broadcast(bias_row[C2:C2 + 1, source].rearrange("p (h d) -> p h d", h=HEADS), 2, 2),
                                  ALU.add)
            source = slice(2 * C, 3 * C)
            dve.tensor_tensor(wqkv[C2:C2 + 1, 2 * C2:3 * C2].rearrange("p (b n) -> p b n", b=2),
                              broadcast(probs_t_ps[C2:C2 + 1, source], 1, 2), broadcast(bias_row[C2:C2 + 1, source], 1, 2),
                              ALU.add).then_inc(setup_dve, 1)
            dve.wait_ge(setup_dve, 3)
            dve.tensor_copy(wqk_r[:, HIGH, :], wqkv[:, 0:2 * C2]).then_inc(setup_dve, 1)
            dve.wait_ge(setup_dve, 4)
            dve.tensor_tensor(wqk_r[:, LOW, :], wqkv[:, 0:2 * C2], wqk_r[:, HIGH, :].bitcast(F32), ALU.subtract
                              ).then_inc(qkv_ok, 1)

            dve.wait_ge(table_in, 16 * TABLE_DMAS)
            wide = bass.AP(pos_in, 0, [[HEADS * (REL * (WIN - 1) + WIN), TOK], [REL * (WIN - 1) + WIN, HEADS],
                                       [REL, WIN], [1, WIN]])
            for part in range(2):
                ins = dve.tensor_copy(pos_all[TOK * part:TOK * part + TOK, :, :, :], wide)
            ins.then_inc(setup_dve, 1)
            dve.wait_ge(setup_dve, 5)
            pos_flat = pos_all[:, :, :, :].rearrange("p h i j -> p (h i j)")
            dve.tensor_copy(pos_high[:, :], pos_flat).then_inc(setup_dve, 1)
            dve.wait_ge(setup_dve, 6)
            for a in range(2):
                dve.tensor_copy(pos[0:TOK, a, :], pos_high[0:TOK, :].bitcast(F32))
                ins = dve.tensor_tensor(pos[TOK:2 * TOK, a, :], pos_flat[TOK:2 * TOK, :],
                                        pos_high[TOK:2 * TOK, :].bitcast(F32), ALU.subtract)
            ins.then_inc(pos_ok, 1)

            def other_weights():
                dve.wait_ge(weights_in, 16 * WEIGHT_DMAS)
                for b in range(2):
                    dve.tensor_scalar(wproj[0:C2, C * b:C * b + C], wproj_in[:, :], window_mask[:, b:b + 1], None, ALU.mult)
                dve.tensor_scalar(wfc1[:, :], wfc1_in[:, :], fc1_gain[:, 0:1], None, ALU.mult).then_inc(setup_dve, 1)
                dve.memset(wfc1_shared[:, :, :].bitcast(F32), 0.0)
                dve.memset(wfc1_low[:, :].bitcast(F32), 0.0)
                dve.memset(normed2[:, :, :, C:C + 1], 1.0)
                dve.memset(normed2[:, :, :, C + 1:PAD], 0.0)
                dve.wait_ge(bias_mm, 2)
                dve.wait_ge(setup_dve, 7)
                dve.tensor_tensor(wfc1[:, :], mixed_ps[:, 0:HID], wfc1[:, :], ALU.add).then_inc(setup_dve, 1)
                dve.wait_ge(setup_dve, 8)
                dve.tensor_copy(wfc1_high[:, :], wfc1[:, :]).then_inc(setup_dve, 1)
                dve.wait_ge(setup_dve, 9)
                for a in range(2):
                    rows = slice(PAD * a, PAD * a + PAD)
                    dve.tensor_tensor(wfc1_low[rows, HID * a:HID * a + HID], wfc1[rows, :],
                                      wfc1_high[rows, :].bitcast(F32), ALU.subtract)
                    source = slice(0, 64) if a else slice(128, HID)
                    ins = dve.tensor_copy(wfc1_shared[:, a, 64 * a:64 * a + 64], wfc1_high[:, source].bitcast(F32))
                ins.then_inc(weights_ok, 1)

            def q_out():
                dve.tensor_tensor(
                    q_blocks[:, :, :, :, :].rearrange("p k a b q -> p (k a) b q"),
                    broadcast(q_ps[0:C2, 0:4 * TOK].rearrange("p (ka q) -> p ka q", q=TOK), 2, 2),
                    broadcast(broadcast(q_mask[:, :], 1, 4), 3, TOK), ALU.mult).then_inc(q_ok, 1)

            def lower(g, k):
                rows = scores_ps[k % 2][:, 0:2 * HEADS * TOK].rearrange("p (r t) -> p r t", t=TOK)
                dve.tensor_reduce(row_top[:, k % 2, :], rows, AX.X, ALU.max).then_inc(max_ok, 1)
                dve.wait_ge(max_ok, g + 1)
                wait(dve, probs_ok, g)
                dve.tensor_tensor(lowered[:, :, :, :].rearrange("p a h t -> p (a h) t"), rows,
                                  broadcast(row_top[:, k % 2, :], 2, TOK), ALU.subtract).then_inc(lowered_ok, 1)

            def normalise(g, k):
                mixed = mixed_ps[:, 0:HEADS * MIX].rearrange("p (h m) -> p h m", h=HEADS)
                dve.reciprocal(inv_sum[:, :, :], mixed[:, :, MIX - 2:MIX]).then_inc(inv_ok, 1)
                dve.wait_ge(inv_ok, g + 1)
                for b in range(2):
                    rows = slice(TOK * b, TOK * b + TOK)
                    own = mixed[rows, :, 2 * HD * b:2 * HD * b + 2 * HD].rearrange("p h (a d) -> p h a d", a=2)
                    ins = dve.tensor_tensor(heads[rows, k % 2, :, :, :].rearrange("p a h d -> p h a d"), own,
                                            broadcast(inv_sum[rows, :, :], 3, HD), ALU.mult)
                ins.then_inc(heads_ok, 1)

            def tokens2_rest(r, half):
                for a in range(2):
                    own, other = slice(PAD * a, PAD * a + PAD), slice(PAD * (1 - a), PAD * (2 - a))
                    wait(dve, tokens2_high_ok, 2 * r + a + 1)
                    ins = dve.tensor_tensor(tokens2_both[other, half, a, :], turn_ps[own, :],
                                            tokens2_both[own, half, a, :].bitcast(F32), ALU.subtract)
                ins.then_inc(tokens2_t_ok, 1)

            def add_proj(n, half):
                tokens = x2_half(n, half)
                bank = (turn_ps, heads_t_ps)[half]
                dve.tensor_tensor(tokens, bank[:, 0:HALF * C2].rearrange("p (j a c) -> p j a c", j=HALF, a=2),
                                  tokens, ALU.add).then_inc(x2_ok, 1)

            def stats_front(n, part):
                if part == 0:
                    wait(dve, small_step, SMALL_STEPS * (n - 1) + 3)
                    wait(dve, x_loaded, 16 * QUADS * (n + 1))
                ins = take_stats(x_groups, (range(STATS_CUT), range(STATS_CUT, GROUPS))[part])
                if part == 1:
                    ins.then_inc(stats_ok, 1)

            def body(n, first, last, more):
                g0 = QUADS * n
                for k in range(QUADS):
                    wait(dve, scores_mm, g0 + k + 1)
                    lower(g0 + k, k)
                    if k == 3 and not first:
                        dve.wait_ge(res_loaded, 64 * n)
                        for half in range(2):
                            dve.wait_ge(proj_mm, 2 * n - 1 + half)
                            add_proj(n - 1, half)
                    if k % 2 == 1 and not (last and k == QUADS - 1):
                        wait(dve, q_mm, 4 * n + k // 2 + 2)
                        q_out()
                    if not (first and k < 2):
                        wait(dve, mixed_mm, g0 + k - 1)
                        normalise(g0 + k - 2, k - 2)
                    if k == 5 and last:
                        tokens2_rest(0, 0)
                    if k == 6 and not last:
                        tokens_low(dve, n + 1, 1).then_inc(tokens_low1, 1)
                    if last and k in (0, 4):
                        if k == 0:
                            dve.wait_ge(small_step, SMALL_STEPS * (BATCHES - 1) + 3)
                        else:
                            dve.wait_ge(small2_step, 3)
                        dve.wait_ge(x2_ok, 2 * (k // 4) + 2)
                        stats_back(k // 4, 0)
                        stats_back(k // 4, 1).then_inc(stats2_ok, 1)
                    if k == 0 and first:
                        stats_front(n + 1, 0)
                    if k == 1 and not last:
                        stats_front(n + 1, 1)
                    if k == QUADS - 1 and more:
                        stats_front(n + 2, 0)

            tokens_low(dve, 0, 0).then_inc(tokens_low0, 1)
            tokens_low(dve, 0, 1).then_inc(tokens_low1, 1)
            dve.wait_ge(q_mm, 1)
            q_out()
            other_weights()
            body(0, True, False, True)
            with dve.Fori(1, BATCHES - 2) as n:
                body(n, False, False, True)
            body(BATCHES - 2, False, False, False)
            body(BATCHES - 1, False, True, False)
            total = QUADS * BATCHES
            for k in (QUADS - 2, QUADS - 1):
                g = total - QUADS + k
                dve.wait_ge(mixed_mm, g + 1)
                normalise(g, k)
                if k == QUADS - 2:
                    tokens2_rest(1, 1)
            dve.wait_ge(small2_step, SMALL_STEPS + 3)
            stats_back(2, 0)
            stats_back(2, 1).then_inc(stats2_ok, 1)
            dve.wait_ge(res_loaded, 64 * BATCHES)
            for half in range(2):
                dve.wait_ge(proj_mm, 2 * BATCHES - 1 + half)
                add_proj(BATCHES - 1, half)

            def add_mlp(n, half):
                tokens = x2_half(n, half)
                dve.tensor_tensor(tokens, fc2_ps[half][:, 0:HALF * C2].rearrange("p (j a c) -> p j a c", j=HALF, a=2),
                                  tokens, ALU.add).then_inc(out_ok, 1)

            def back(n, first, last, more):
                for half in range(2):
                    r = 2 * n + half
                    if not (first and half == 0) and not (last and half == 1):
                        tokens2_rest(r + 1, 1 - half)
                    if half == 0 and more and not first:
                        wait(dve, small2_step, SMALL_STEPS * (n + 1) + 3)
                        stats_back(n + 2, 0)
                        stats_back(n + 2, 1).then_inc(stats2_ok, 1)
                    if half == 1:
                        wait(dve, normed2_ok, 2 * n + 2)
                        residual = x2_batch(n).rearrange("p a j c -> p (a j) c")
                        dve.tensor_tensor(residual, residual, broadcast(fc2_bias[:, :], 1, GROUPS),
                                          ALU.add).then_inc(biased2_ok, 1)
                    if not (first and half == 0):
                        if half == 1:
                            wait(dve, biased2_ok, n + 1)
                        wait(dve, fc2_mm, r)
                        add_mlp(n if half else n - 1, 1 - half)

            back(0, True, False, True)
            with dve.Fori(1, BATCHES - 2) as n:
                back(n, False, False, True)
            back(BATCHES - 2, False, False, False)
            back(BATCHES - 1, False, True, False)
            dve.wait_ge(fc2_mm, 2 * BATCHES)
            add_mlp(BATCHES - 1, 1)


_P = "L0_conv_"
_INS = ["x"] + [_P + n for n in ("norm1_g", "norm1_b", "qkv_w", "qkv_b", "proj_w", "proj_b", "rel_bias_table",
                                 "norm2_g", "norm2_b", "fc1_w", "fc1_b", "fc2_w", "fc2_b")]


def kernel(**inputs):
    import concourse.bacc as bacc
    from concourse.bass_utils import run_bass_kernel_spmd

    nc = bacc.Bacc("TRN2", target_bir_lowering=False, num_devices=1)
    arrays, args = {}, []
    for name in _INS:
        a = np.asarray(inputs[name])
        if name.endswith("rel_bias_table"):
            a = a[::-1].T
        a = np.ascontiguousarray(a)
        arrays[f"in_{name}"] = a
        args.append(nc.dram_tensor(f"in_{name}", a.shape, mybir.dt.from_np(a.dtype), kind="ExternalInput").ap())
    args.append(nc.dram_tensor("out", (IMAGES, H, W, C), F32, kind="ExternalOutput").ap())
    swin_block(nc, *args)
    r = run_bass_kernel_spmd(nc, [arrays], core_ids=[0])
    return r.results[0]["out"]
```
